# Optimizing a Trainium2 kernel written in Bass

```python
import numpy as np
import jax
import jax.numpy as jnp

def _softmax(x, axis=-1):
    return jax.nn.softmax(x, axis=axis)

def _gelu(x):
    return jax.nn.gelu(x, approximate=True)

def _silu(x):
    return jax.nn.silu(x)

def _sigmoid(x):
    return jax.nn.sigmoid(x)

def _layernorm(x, axis=-1, eps=1e-05):
    m = jnp.mean(x, axis=axis, keepdims=True)
    v = jnp.var(x, axis=axis, keepdims=True)
    return (x - m) / jnp.sqrt(v + eps)

def _scatter_add(tgt, idx, src, axis=0):
    return tgt.at[idx].add(src)

def _segment_sum(src, seg, n):
    return jax.ops.segment_sum(src, seg, n)
kernel_name = 'mk_hybrid_d1_jaxref_r8_b13816'

def setup_inputs(seed: int=0):
    np.random.seed(seed)
    _w = jnp.asarray

    def _L0_attn_a_setup():
        import jax, jax.numpy as jnp
        import numpy as np
        import math
        N_HEADS = 4
        N_KV_GROUPS = 1
        HEAD_DIM = 32
        SLIDING_WINDOW = 64
        ROPE_BASE = 1000000.0
        EPS = 1e-06

        def _rmsnorm(x, gamma):
            ms = jnp.mean(jnp.square(x), axis=-1, keepdims=True)
            return x * jax.lax.rsqrt(ms + EPS) * gamma

        def _rope_tables(T, head_dim, dtype):
            inv_freq = 1.0 / ROPE_BASE ** (jnp.arange(0, head_dim, 2, dtype=jnp.float32) / head_dim)
            t = jnp.arange(T, dtype=jnp.float32)
            freqs = jnp.outer(t, inv_freq)
            return (jnp.cos(freqs).astype(dtype), jnp.sin(freqs).astype(dtype))

        def _apply_rope(x, cos, sin):
            x0 = x[..., 0::2]
            x1 = x[..., 1::2]
            c = cos[None, :, None, :]
            s = sin[None, :, None, :]
            even = x0 * c - x1 * s
            odd = x0 * s + x1 * c
            return jnp.stack((even, odd), axis=-1).reshape(x.shape)
        key = jax.random.key(seed)
        ks = jax.random.split(key, 5)
        B, T, C = (2, 512, 128)
        scale = 0.02
        return {'x': jax.random.normal(ks[0], (B, T, C), dtype=jnp.float32), 'Wq': jax.random.normal(ks[1], (C, C), dtype=jnp.float32) * scale, 'Wk': jax.random.normal(ks[2], (N_KV_GROUPS * HEAD_DIM, C), dtype=jnp.float32) * scale, 'Wv': jax.random.normal(ks[3], (N_KV_GROUPS * HEAD_DIM, C), dtype=jnp.float32) * scale, 'Wo': jax.random.normal(ks[4], (C, C), dtype=jnp.float32) * scale, 'q_gamma': jnp.ones((HEAD_DIM,), dtype=jnp.float32), 'k_gamma': jnp.ones((HEAD_DIM,), dtype=jnp.float32)}
    _L0_attn_a_in = _L0_attn_a_setup()

    def _L0_attn_b_setup():
        import jax, jax.numpy as jnp
        import numpy as np
        NUM_HEADS = 16
        WINDOW = 32

        def _sliding_window_attn(x, wq, wk, wv, wo):
            B, S, D = x.shape
            H, W = (NUM_HEADS, WINDOW)
            Dh = D // H
            nb = S // W

            def proj(w):
                y = (x @ w.T).reshape(B, nb, W, H, Dh)
                return y.transpose(0, 3, 1, 2, 4)
            q = proj(wq)
            k = proj(wk)
            v = proj(wv)
            zpad = jnp.zeros((B, H, 1, W, Dh), dtype=x.dtype)
            kpad = jnp.concatenate([zpad, k], axis=2)
            vpad = jnp.concatenate([zpad, v], axis=2)
            k2 = jnp.concatenate([kpad[:, :, :-1], kpad[:, :, 1:]], axis=3)
            v2 = jnp.concatenate([vpad[:, :, :-1], vpad[:, :, 1:]], axis=3)
            scores = jnp.einsum('bhjqd,bhjkd->bhjqk', q, k2) / jnp.sqrt(jnp.asarray(Dh, dtype=x.dtype))
            qi = jnp.arange(W)[:, None]
            ki = jnp.arange(2 * W)[None, :]
            band = (ki >= qi + 1) & (ki <= qi + W)
            kpos_ok = (jnp.arange(nb)[:, None, None] - 1) * W + ki[None] >= 0
            mask = band[None] & kpos_ok
            neg = jnp.finfo(scores.dtype).min
            scores = jnp.where(mask[None, None], scores, neg)
            attn = jax.nn.softmax(scores, axis=-1)
            out = jnp.einsum('bhjqk,bhjkd->bhjqd', attn, v2)
            out = out.transpose(0, 2, 3, 1, 4).reshape(B, S, D)
            return out @ wo.T
        key = jax.random.key(seed)
        k1, k2, k3, k4, k5 = jax.random.split(key, 5)
        B, S, D = (2, 512, 128)
        scale = 0.02
        return {'x': jax.random.normal(k1, (B, S, D), dtype=jnp.float32), 'wq': jax.random.normal(k2, (D, D), dtype=jnp.float32) * scale, 'wk': jax.random.normal(k3, (D, D), dtype=jnp.float32) * scale, 'wv': jax.random.normal(k4, (D, D), dtype=jnp.float32) * scale, 'wo': jax.random.normal(k5, (D, D), dtype=jnp.float32) * scale}
    _L0_attn_b_in = _L0_attn_b_setup()

    def _L0_ffn_setup():
        import jax, jax.numpy as jnp
        import numpy as np
        B, T, DIM = (2, 256, 128)
        H, DH, E, K = (16, 64, 8, 2)
        key = jax.random.key(seed)
        ks = jax.random.split(key, 7)
        s = 0.02
        return {'x': jax.random.normal(ks[0], (B, T, DIM), jnp.float32), 'Wq': jax.random.normal(ks[1], (H, DH, DIM), jnp.float32) * s, 'Wk': jax.random.normal(ks[2], (H, DH, DIM), jnp.float32) * s, 'Wv': jax.random.normal(ks[3], (E, DH, DIM), jnp.float32) * s, 'Ws': jax.random.normal(ks[4], (H, E, DIM), jnp.float32) * s, 'Wd': jax.random.normal(ks[5], (H, E, DIM), jnp.float32) * s, 'Wo': jax.random.normal(ks[6], (E, DIM, DH), jnp.float32) * s}
    _L0_ffn_in = _L0_ffn_setup()
    _d = {'L0_attn_a_x': _L0_attn_a_in['x'], 'L0_attn_a_Wq': _L0_attn_a_in['Wq'], 'L0_attn_a_Wk': _L0_attn_a_in['Wk'], 'L0_attn_a_Wv': _L0_attn_a_in['Wv'], 'L0_attn_a_Wo': _L0_attn_a_in['Wo'], 'L0_attn_a_q_gamma': _L0_attn_a_in['q_gamma'], 'L0_attn_a_k_gamma': _L0_attn_a_in['k_gamma'], 'L0_attn_b_wq': _L0_attn_b_in['wq'], 'L0_attn_b_wk': _L0_attn_b_in['wk'], 'L0_attn_b_wv': _L0_attn_b_in['wv'], 'L0_attn_b_wo': _L0_attn_b_in['wo'], 'L0_ffn_Wq': _L0_ffn_in['Wq'], 'L0_ffn_Wk': _L0_ffn_in['Wk'], 'L0_ffn_Wv': _L0_ffn_in['Wv'], 'L0_ffn_Ws': _L0_ffn_in['Ws'], 'L0_ffn_Wd': _L0_ffn_in['Wd'], 'L0_ffn_Wo': _L0_ffn_in['Wo']}
    _x0 = _d['L0_attn_a_x']
    _d['L0_attn_a_x'] = jax.random.normal(jax.random.fold_in(jax.random.key(seed), 1), (2, 1024, 128), dtype=_x0.dtype)
    del _x0
    return _d

def reference(L0_attn_a_x, L0_attn_a_Wq, L0_attn_a_Wk, L0_attn_a_Wv, L0_attn_a_Wo, L0_attn_a_q_gamma, L0_attn_a_k_gamma, L0_attn_b_wq, L0_attn_b_wk, L0_attn_b_wv, L0_attn_b_wo, L0_ffn_Wq, L0_ffn_Wk, L0_ffn_Wv, L0_ffn_Ws, L0_ffn_Wd, L0_ffn_Wo):

    def _L0_attn_a_ref(x, Wq, Wk, Wv, Wo, q_gamma, k_gamma):
        import jax, jax.numpy as jnp
        import numpy as np
        import math
        N_HEADS = 4
        N_KV_GROUPS = 1
        HEAD_DIM = 32
        SLIDING_WINDOW = 64
        ROPE_BASE = 1000000.0
        EPS = 1e-06

        def _rmsnorm(x, gamma):
            ms = jnp.mean(jnp.square(x), axis=-1, keepdims=True)
            return x * jax.lax.rsqrt(ms + EPS) * gamma

        def _rope_tables(T, head_dim, dtype):
            inv_freq = 1.0 / ROPE_BASE ** (jnp.arange(0, head_dim, 2, dtype=jnp.float32) / head_dim)
            t = jnp.arange(T, dtype=jnp.float32)
            freqs = jnp.outer(t, inv_freq)
            return (jnp.cos(freqs).astype(dtype), jnp.sin(freqs).astype(dtype))

        def _apply_rope(x, cos, sin):
            x0 = x[..., 0::2]
            x1 = x[..., 1::2]
            c = cos[None, :, None, :]
            s = sin[None, :, None, :]
            even = x0 * c - x1 * s
            odd = x0 * s + x1 * c
            return jnp.stack((even, odd), axis=-1).reshape(x.shape)
        B, T, C = x.shape
        H, G, hd = (N_HEADS, N_KV_GROUPS, HEAD_DIM)
        rep = H // G
        q = (x @ Wq.T).reshape(B, T, H, hd)
        k = (x @ Wk.T).reshape(B, T, G, hd)
        v = (x @ Wv.T).reshape(B, T, G, hd)
        q = _rmsnorm(q, q_gamma)
        k = _rmsnorm(k, k_gamma)
        cos, sin = _rope_tables(T, hd, q.dtype)
        q = _apply_rope(q, cos, sin)
        k = _apply_rope(k, cos, sin)
        q = q.transpose(0, 2, 1, 3)
        k = k.transpose(0, 2, 1, 3)
        v = v.transpose(0, 2, 1, 3)
        k = jnp.repeat(k, rep, axis=1)
        v = jnp.repeat(v, rep, axis=1)
        scores = jnp.einsum('bhqd,bhkd->bhqk', q, k) / math.sqrt(hd)
        i = jnp.arange(T)[:, None]
        j = jnp.arange(T)[None, :]
        allowed = (j <= i) & (j >= i - SLIDING_WINDOW)
        scores = jnp.where(allowed, scores, -jnp.inf)
        attn = jax.nn.softmax(scores, axis=-1)
        out = jnp.einsum('bhqk,bhkd->bhqd', attn, v)
        out = out.transpose(0, 2, 1, 3).reshape(B, T, C)
        return out @ Wo.T

    def _L0_attn_b_ref(x, wq, wk, wv, wo):
        import jax, jax.numpy as jnp
        import numpy as np
        NUM_HEADS = 16
        WINDOW = 32

        def _sliding_window_attn(x, wq, wk, wv, wo):
            B, S, D = x.shape
            H, W = (NUM_HEADS, WINDOW)
            Dh = D // H
            nb = S // W

            def proj(w):
                y = (x @ w.T).reshape(B, nb, W, H, Dh)
                return y.transpose(0, 3, 1, 2, 4)
            q = proj(wq)
            k = proj(wk)
            v = proj(wv)
            zpad = jnp.zeros((B, H, 1, W, Dh), dtype=x.dtype)
            kpad = jnp.concatenate([zpad, k], axis=2)
            vpad = jnp.concatenate([zpad, v], axis=2)
            k2 = jnp.concatenate([kpad[:, :, :-1], kpad[:, :, 1:]], axis=3)
            v2 = jnp.concatenate([vpad[:, :, :-1], vpad[:, :, 1:]], axis=3)
            scores = jnp.einsum('bhjqd,bhjkd->bhjqk', q, k2) / jnp.sqrt(jnp.asarray(Dh, dtype=x.dtype))
            qi = jnp.arange(W)[:, None]
            ki = jnp.arange(2 * W)[None, :]
            band = (ki >= qi + 1) & (ki <= qi + W)
            kpos_ok = (jnp.arange(nb)[:, None, None] - 1) * W + ki[None] >= 0
            mask = band[None] & kpos_ok
            neg = jnp.finfo(scores.dtype).min
            scores = jnp.where(mask[None, None], scores, neg)
            attn = jax.nn.softmax(scores, axis=-1)
            out = jnp.einsum('bhjqk,bhjkd->bhjqd', attn, v2)
            out = out.transpose(0, 2, 3, 1, 4).reshape(B, S, D)
            return out @ wo.T
        return _sliding_window_attn(x, wq, wk, wv, wo)

    def _L0_ffn_ref(x, Wq, Wk, Wv, Ws, Wd, Wo):
        import jax, jax.numpy as jnp
        import numpy as np
        B, T, DIM = (2, 256, 128)
        H, DH, E, K = (16, 64, 8, 2)
        scale = DH ** (-0.5)
        q = jnp.einsum('btc,hdc->bhtd', x, Wq)
        k = jnp.einsum('btc,hdc->bhtd', x, Wk)
        gate_v = jnp.einsum('btc,hec->bthe', x, Ws)
        w, sel = jax.lax.top_k(gate_v, K)
        wsig = jax.nn.sigmoid(w)
        oh = jax.nn.one_hot(sel, E, dtype=x.dtype)
        mix_v = jnp.einsum('bthk,bthke->bthe', wsig, oh)
        proj_v = jnp.einsum('btc,edc->bted', x, Wv)
        v = jnp.einsum('bthe,bted->bhtd', mix_v, proj_v)
        scores = jnp.einsum('bhid,bhjd->bhij', q * scale, k)
        probs = jax.nn.softmax(scores, axis=-1)
        attn = jnp.einsum('bhij,bhjd->bihd', probs, v)
        gate_o = jnp.einsum('btc,hec->bthe', x, Wd)
        _, sel_o = jax.lax.top_k(gate_o, K)
        mask_o = jax.nn.one_hot(sel_o, E, dtype=x.dtype).sum(axis=3)
        res = jnp.einsum('bthe,bthd,efd->bthf', mask_o, attn, Wo)
        return res.sum(axis=2)
    x = L0_attn_a_x
    x = x + _L0_attn_a_ref(_layernorm(x, axis=-1), L0_attn_a_Wq, L0_attn_a_Wk, L0_attn_a_Wv, L0_attn_a_Wo, L0_attn_a_q_gamma, L0_attn_a_k_gamma)
    x = x + _L0_ffn_ref(_layernorm(x, axis=-1), L0_ffn_Wq, L0_ffn_Wk, L0_ffn_Wv, L0_ffn_Ws, L0_ffn_Wd, L0_ffn_Wo)
    x = x + _L0_attn_b_ref(_layernorm(x, axis=-1), L0_attn_b_wq, L0_attn_b_wk, L0_attn_b_wv, L0_attn_b_wo)
    x = x + _L0_ffn_ref(_layernorm(x, axis=-1), L0_ffn_Wq, L0_ffn_Wk, L0_ffn_Wv, L0_ffn_Ws, L0_ffn_Wd, L0_ffn_Wo)
    return x

_drawn_inputs = setup_inputs


def setup_inputs(seed=0):
    import zlib

    import numpy as np

    out = dict(_drawn_inputs(seed))
    spreads = {'L0_attn_a_q_gamma': (1.0, 0.6), 'L0_attn_a_k_gamma': (1.0, 0.6)}
    factors = {'L0_attn_a_Wq': 6.399,
     'L0_attn_a_Wk': 6.334,
     'L0_attn_a_Wv': 4.909,
     'L0_attn_a_Wo': 4.926,
     'L0_attn_b_wq': 8.0,
     'L0_attn_b_wk': 8.0,
     'L0_attn_b_wv': 5.922,
     'L0_attn_b_wo': 5.933,
     'L0_ffn_Wq': 8.0,
     'L0_ffn_Wk': 8.0,
     'L0_ffn_Ws': 2.758,
     'L0_ffn_Wd': 3.212}
    for name, (base, spread) in spreads.items():
        noise = np.random.default_rng([zlib.crc32(name.encode()), seed]).standard_normal(out[name].shape)
        drawn = base * np.exp(spread * noise) if base else spread * noise
        out[name] = jnp.asarray(drawn.astype(out[name].dtype))
    for name, factor in factors.items():
        out[name] = (out[name] * factor).astype(out[name].dtype)
    return out
```

```python
from contextlib import ExitStack

import numpy as np

import concourse.bass as bass
from concourse import mybir

ALU = mybir.AluOpType
ACT = mybir.ActivationFunctionType
AX_X = mybir.AxisListType.X
F32 = mybir.dt.float32
F32R = mybir.dt.float32r
BF16 = mybir.dt.bfloat16

P = 128
C = 128
LN_EPS = 1e-5
RMS_EPS = 1e-6
NEG = -1e30


class Signal:

    def __init__(self, ctx, nc, name):
        self.sem = ctx.enter_context(nc.semaphore(name))
        self.base = 0

    def at(self, k):
        return self.base + k


class Signals:

    def __init__(self, ctx, nc):
        self.ctx, self.nc, self.all = ctx, nc, {}

    def __call__(self, name):
        if name not in self.all:
            self.all[name] = Signal(self.ctx, self.nc, name)
        return self.all[name]

    def close(self, **made):
        for name, n in made.items():
            self.all[name].base += n


def link(eng, sig, ins):
    ins.then_inc(sig.sem, 1)
    sig.base += 1
    eng.wait_ge(sig.sem, sig.base)


def over(ap, n):
    return ap.unsqueeze(len(ap.shape)).to_broadcast(list(ap.shape) + [n])


def over_mid(ap, n):
    return ap.unsqueeze(1).to_broadcast([ap.shape[0], n] + list(ap.shape[1:]))


def turn(pe, out, block, ident):
    return pe.matmul(out, block, ident, start=True, stop=True)


def layernorm_vector(v, S, X, T):
    chain = S("dve_chain")
    NT = X.shape[1]
    link(v, chain, v.tensor_reduce(T["sum"][:, 0:NT], X, AX_X, ALU.add))
    link(v, chain, v.tensor_scalar(T["sum"][:, 0:NT], T["sum"][:, 0:NT], 1.0 / C, None, ALU.mult))
    v.tensor_tensor(T["xc"][:], X, over(T["sum"][:, 0:NT], C), ALU.subtract).then_inc(S("centered").sem, 1)
    v.wait_ge(S("squared").sem, S("squared").at(1))
    link(v, chain, v.tensor_reduce(T["var"][:, 0:NT], T["sq"][:], AX_X, ALU.add))
    v.tensor_scalar(T["var"][:, 0:NT], T["var"][:, 0:NT], 1.0 / C, LN_EPS, ALU.mult, ALU.add).then_inc(
        S("var_ready").sem, 1)
    v.wait_ge(S("std_ready").sem, S("std_ready").at(1))
    link(v, chain, v.reciprocal(T["rstd"][:, 0:NT], T["std"][:, 0:NT]))
    v.tensor_tensor(T["xn"][:], T["xc"][:], over(T["rstd"][:, 0:NT], C), ALU.mult).then_inc(S("normed").sem, 1)


def layernorm_scalar(a, S, NT, T):
    a.wait_ge(S("centered").sem, S("centered").at(1))
    a.activation(T["sq"][:], T["xc"][:], ACT.Square).then_inc(S("squared").sem, 1)
    a.wait_ge(S("var_ready").sem, S("var_ready").at(1))
    a.activation(T["std"][:, 0:NT], T["var"][:, 0:NT], ACT.Sqrt).then_inc(S("std_ready").sem, 1)


def build(nc, IN, out):
    x_in = IN["L0_attn_a_x"]
    B, T, _ = x_in.shape
    NT = T // P
    HF, DH, _ = IN["L0_ffn_Wq"].shape
    E = IN["L0_ffn_Wv"].shape[0]
    ED = E * DH
    NEC = ED // P
    HE = HF * E
    FFN_SCALE = float(DH) ** -0.5

    with ExitStack() as ctx:
        def sb(name, shape, dt=F32, c=ctx):
            return c.enter_context(nc.sbuf_tensor(name, shape, dt))

        S = Signals(ctx, nc)
        ps = ctx.enter_context(nc.psum_tensor("ps", [P, 8, 512], F32))

        X = sb("X", [P, B * NT, C])
        ident = sb("ident", [P, P])
        identb = sb("identb", [P, P], BF16)
        WQK = sb("WQK", [P, HF, 2, 2 * DH], F32R)
        WVG = sb("WVG", [P, 2, ED + 2 * HE], F32R)
        WOF = sb("WOF", [P, NEC, C])
        GAM = sb("GAM", [P, 5, 32])
        COS = sb("COS", [P, NT, 16])
        SIN = sb("SIN", [P, NT, 16])

        A_H, A_HD, A_QB, A_LO = 4, 32, 64, 0
        B_H, B_HD, B_QB, B_LO = 16, 8, 32, 1
        WA = sb("WA", [P, 192])
        WOA = sb("WOA", [P, C])
        WB = sb("WB", [P, 3 * C])
        WOB = sb("WOB", [P, C])
        masks = {"a": sb("mask_a", [P, 2, 2 * A_QB], BF16), "b": sb("mask_b", [P, 2, 2 * B_QB], BF16)}
        heads = {"a": sb("heads_a", [P, A_H]), "b": sb("heads_b", [P, B_H])}

        with ExitStack() as c:
            raw = sb("raw", [P, 30, C], F32, c)
            Q0, K0, V0, S0, D0, O0, AQ, AKV, AO, BQ = 0, 8, 16, 20, 21, 22, 26, 27, 28, 29
            rawb = sb("rawb", [P, 3, C], F32, c)
            loads = []

            def load(dst, src):
                loads.append((dst, src))

            load(X[:, 0:NT, :], x_in[0].rearrange("(n p) c -> p n c", p=P))
            load(raw[:, Q0:Q0 + 8, :], IN["L0_ffn_Wq"].rearrange("h d c -> (h d) c").rearrange("(n p) c -> p n c", p=P))
            load(raw[:, K0:K0 + 8, :], IN["L0_ffn_Wk"].rearrange("h d c -> (h d) c").rearrange("(n p) c -> p n c", p=P))
            load(raw[:, V0:V0 + 4, :], IN["L0_ffn_Wv"].rearrange("h d c -> (h d) c").rearrange("(n p) c -> p n c", p=P))
            load(raw[:, S0, :], IN["L0_ffn_Ws"].rearrange("h e c -> (h e) c"))
            load(raw[:, D0, :], IN["L0_ffn_Wd"].rearrange("h e c -> (h e) c"))
            load(raw[:, O0:O0 + 4, :].rearrange("f n (e d) -> f (n e) d", d=DH), IN["L0_ffn_Wo"].rearrange("e f d -> f e d"))
            load(raw[:, AQ, :], IN["L0_attn_a_Wq"])
            load(raw[0:32, AKV, :], IN["L0_attn_a_Wk"])
            load(raw[32:64, AKV, :], IN["L0_attn_a_Wv"])
            load(raw[:, AO, :], IN["L0_attn_a_Wo"])
            load(raw[:, BQ, :], IN["L0_attn_b_wq"])
            load(rawb[:, 0, :], IN["L0_attn_b_wk"])
            load(rawb[:, 1, :], IN["L0_attn_b_wv"])
            load(rawb[:, 2, :], IN["L0_attn_b_wo"])
            for n in range(4):
                load(GAM[:, n, :], IN["L0_attn_a_q_gamma"].rearrange("(a d) -> a d", a=1).to_broadcast([P, 32]))
            load(GAM[:, 4, :], IN["L0_attn_a_k_gamma"].rearrange("(a d) -> a d", a=1).to_broadcast([P, 32]))
            load(COS[:], IN["rope_cos"].rearrange("(n p) f -> p n f", p=P))
            load(SIN[:], IN["rope_sin"].rearrange("(n p) f -> p n f", p=P))
            load(X[:, NT:2 * NT, :], x_in[1].rearrange("(n p) c -> p n c", p=P))
            n_loads = len(loads)
            loaded, made, turned, split, moved = S("loaded"), S("const_made"), S("turned"), S("split_hi"), S("bank_freed")

            with nc.Block() as block:
                @block.sync
                def _(sp):
                    for dst, src in loads[0::2]:
                        sp.dma_start(dst, src).then_inc(loaded.sem, 16)

                @block.gpsimd
                def _(g):
                    chain = S("pool_chain")
                    link(g, chain, g.memset(ident[:], 0.0))
                    link(g, chain, g.affine_select(out=ident[:], in_=ident[:], compare_op=ALU.not_equal, fill=1.0,
                                                   base=0, pattern=[[-1, P]], channel_multiplier=1))
                    g.tensor_copy(identb[:], ident[:]).then_inc(made.sem, 1)
                    for key, QB, H, HD, LO in (("a", A_QB, A_H, A_HD, A_LO), ("b", B_QB, B_H, B_HD, B_LO)):
                        m, KB = masks[key], 2 * QB
                        link(g, chain, g.memset(m[:], 0.0))
                        for j in range(P // QB):
                            v = m[QB * j:QB * (j + 1), :, :]
                            link(g, chain, g.affine_select(out=v, in_=v, compare_op=ALU.is_ge, fill=NEG, base=-LO,
                                                           pattern=[[0, 2], [1, KB]], channel_multiplier=-1))
                            link(g, chain, g.affine_select(out=v, in_=v, compare_op=ALU.is_ge, fill=NEG, base=QB,
                                                           pattern=[[0, 2], [-1, KB]], channel_multiplier=1))
                        v = m[0:QB, 1, :]
                        link(g, chain, g.affine_select(out=v, in_=v, compare_op=ALU.is_ge, fill=NEG, base=-QB,
                                                       pattern=[[1, KB]], channel_multiplier=0))
                        h = heads[key]
                        link(g, chain, g.memset(h[:], 1.0))
                        link(g, chain, g.affine_select(out=h[:], in_=h[:], compare_op=ALU.is_ge, fill=0.0, base=0,
                                                       pattern=[[-HD, H]], channel_multiplier=1))
                        link(g, chain, g.affine_select(out=h[:], in_=h[:], compare_op=ALU.is_ge, fill=0.0, base=HD - 1,
                                                       pattern=[[HD, H]], channel_multiplier=-1))

                banks = [[(Q0 + n) for n in range(4)], [(Q0 + 4 + n) for n in range(4)],
                         [(K0 + n) for n in range(4)], [(K0 + 4 + n) for n in range(4)],
                         [(V0 + n) for n in range(4)], [S0, D0, AQ, AO], [(O0 + n) for n in range(4)],
                         [BQ, "wk", "wv", "wo"]]

                @block.tensor
                def _(pe):
                    pe.wait_ge(loaded.sem, loaded.at(16 * n_loads))
                    pe.wait_ge(made.sem, made.at(1))
                    for b, blocks in enumerate(banks):
                        for n, r in enumerate(blocks):
                            src = rawb[:, ("wk", "wv", "wo").index(r), :] if isinstance(r, str) else raw[:, r, :]
                            m = turn(pe, ps[:, b, n * P:(n + 1) * P], src, ident[:])
                        m.then_inc(turned.sem, 1)
                    pe.wait_ge(moved.sem, moved.at(1))
                    turn(pe, ps[:, 0, 0:64], raw[0:64, AKV, :], ident[0:64, 0:64]).then_inc(turned.sem, 1)

                @block.scalar
                def _(a):
                    for dst, src in loads[1::2]:
                        a.dma_start(dst, src).then_inc(loaded.sem, 16)
                    for b in range(4):
                        a.wait_ge(turned.sem, turned.at(b + 1))
                        dst = WQK[:, 8 * (b % 2):8 * (b % 2) + 8, 0, DH * (b // 2):DH * (b // 2) + DH]
                        a.activation(dst, ps[:, b, :].rearrange("c (h d) -> c h d", d=DH), ACT.Copy).then_inc(split.sem, 1)
                    a.wait_ge(turned.sem, turned.at(5))
                    a.activation(WVG[:, 0, 0:ED], ps[:, 4, :], ACT.Copy).then_inc(split.sem, 1)
                    a.wait_ge(turned.sem, turned.at(6))
                    a.activation(WVG[:, 0, ED:], ps[:, 5, 0:2 * HE], ACT.Copy).then_inc(split.sem, 1)

                @block.vector
                def _(v):
                    for b in range(4):
                        v.wait_ge(split.sem, split.at(b + 1))
                        hi = WQK[:, 8 * (b % 2):8 * (b % 2) + 8, 0, DH * (b // 2):DH * (b // 2) + DH]
                        lo = WQK[:, 8 * (b % 2):8 * (b % 2) + 8, 1, DH * (b // 2):DH * (b // 2) + DH]
                        d = v.tensor_tensor(lo, ps[:, b, :].rearrange("c (h d) -> c h d", d=DH), hi.bitcast(F32), ALU.subtract)
                        if b == 0:
                            d.then_inc(moved.sem, 1)
                    v.wait_ge(split.sem, split.at(5))
                    v.tensor_tensor(WVG[:, 1, 0:ED], ps[:, 4, :], WVG[:, 0, 0:ED].bitcast(F32), ALU.subtract)
                    v.wait_ge(split.sem, split.at(6))
                    v.tensor_tensor(WVG[:, 1, ED:], ps[:, 5, 0:2 * HE], WVG[:, 0, ED:].bitcast(F32), ALU.subtract)
                    v.tensor_copy(WA[:, 0:C], ps[:, 5, 2 * P:3 * P])
                    v.tensor_copy(WOA[:], ps[:, 5, 3 * P:4 * P])
                    v.wait_ge(turned.sem, turned.at(7))
                    v.tensor_copy(WOF[:], ps[:, 6, :].rearrange("p (n f) -> p n f", n=NEC))
                    v.wait_ge(turned.sem, turned.at(8))
                    v.tensor_copy(WB[:], ps[:, 7, 0:3 * P])
                    v.tensor_copy(WOB[:], ps[:, 7, 3 * P:4 * P])
                    v.wait_ge(turned.sem, turned.at(9))
                    v.tensor_copy(WA[:, C:C + 64], ps[:, 0, 0:64])
            S.close(loaded=16 * n_loads, const_made=1, turned=9, split_hi=6, bank_freed=1)

        for b in range(B):
            Xb = X[:, b * NT:(b + 1) * NT, :]
            windowed(nc, S, ps, Xb, ident, identb, WA, WOA, masks["a"], heads["a"], H=A_H, HD=A_HD, QB=A_QB,
                     tag=f"a{b}", rope=(GAM, COS, SIN))
            ffn(nc, S, ps, Xb, ident, WQK, WVG, WOF, HF, DH, E, FFN_SCALE, tag=f"f{b}")
            windowed(nc, S, ps, Xb, ident, identb, WB, WOB, masks["b"], heads["b"], H=B_H, HD=B_HD, QB=B_QB,
                     tag=f"b{b}", rope=None)
            ffn(nc, S, ps, Xb, ident, WQK, WVG, WOF, HF, DH, E, FFN_SCALE, tag=f"g{b}")
            with nc.Block() as block:
                @block.sync
                def _(sp):
                    sp.dma_start(out[b].rearrange("(n p) c -> p n c", p=P), Xb).then_inc(S("stored").sem, 16)
                    sp.wait_ge(S("stored").sem, S("stored").at(16))
            S.close(stored=16)


def ln_tiles(sb, tag, NT, c):
    T = {n: sb(f"{n}_{tag}", [P, NT, C], F32, c) for n in ("xc", "sq", "xn")}
    T |= {n: sb(f"{n}_{tag}", [P, 8], F32, c) for n in ("sum", "var", "std", "rstd")}
    return T


def windowed(nc, S, ps, X, ident, identb, W, WO, mask, heads, H, HD, QB, tag, rope):
    NT = X.shape[1]
    J = P // QB
    KB = 2 * QB
    HC = P // KB
    NCH = H // HC
    CD = HC * HD
    NB = NT * J
    shared_kv = rope is not None
    NQKV = W.shape[1]
    scale = float(HD) ** -0.5
    SH = 512 // KB
    NS = H // SH
    VW = HD if shared_kv else C

    def sb(name, shape, dt=F32, c=None):
        return c.enter_context(nc.sbuf_tensor(name, shape, dt))

    with ExitStack() as ctx:
        QKV = sb(f"QKV_{tag}", [P, NT, NQKV], F32, ctx)
        QT = sb(f"QT_{tag}", [P, NT * P], F32, ctx)
        KT = sb(f"KT_{tag}", [P, QB + NT * P], F32, ctx)
        KE = sb(f"KE_{tag}", [P, H, QB + NT * P], F32, ctx)
        V2 = sb(f"V2_{tag}", [P, NB + 1, VW], F32, ctx)
        AOUT = sb(f"AOUT_{tag}", [P, NT, C], F32, ctx)

        with ExitStack() as c:
            T = ln_tiles(sb, tag, NT, c)
            XT = sb(f"XT_{tag}", [P, NT * P], F32, c)
            normed, turned, copied, projected = S("normed"), S("turned"), S("turned_copied"), S("projected")
            NH5 = H + 1
            if rope:
                GAM, COS, SIN = rope
                rms = sb(f"rms_{tag}", [P, 4, NT * NH5], F32, c)
                sq5 = sb(f"sq5_{tag}", [P, NT, NH5 * HD], F32, c)
                rn = sb(f"rn_{tag}", [P, NT, NH5 * HD], F32, c)
                r1 = sb(f"r1_{tag}", [P, NT, NH5, HD // 2], F32, c)
                r2 = sb(f"r2_{tag}", [P, NT, NH5, HD // 2], F32, c)

            with nc.Block() as block:
                @block.vector
                def _(v):
                    layernorm_vector(v, S, X, T)
                    for n in range(NT):
                        v.wait_ge(projected.sem, projected.at(n + 1))
                        v.tensor_copy(QKV[:, n, :], ps[:, 2 + n % 6, 0:NQKV]).then_inc(S("qkv_stored").sem, 1)
                    if rope:
                        chain = S("dve_chain")
                        v.wait_ge(S("qkv_stored").sem, S("qkv_stored").at(NT))
                        v.wait_ge(S("rms_squared").sem, S("rms_squared").at(1))
                        link(v, chain, v.tensor_reduce(rms[:, 0, :], sq5[:].rearrange("p n (h d) -> p (n h) d", d=HD),
                                                       AX_X, ALU.add))
                        v.tensor_scalar(rms[:, 1, :], rms[:, 0, :], 1.0 / HD, RMS_EPS, ALU.mult, ALU.add).then_inc(
                            S("rms_sum").sem, 1)
                        v.wait_ge(S("rms_root").sem, S("rms_root").at(1))
                        link(v, chain, v.reciprocal(rms[:, 3, :], rms[:, 2, :]))
                        QK5 = QKV[:, :, 0:NH5 * HD]
                        link(v, chain, v.tensor_tensor(
                            rn[:].rearrange("p n (h d) -> p n h d", d=HD), QK5.rearrange("p n (h d) -> p n h d", d=HD),
                            over(rms[:, 3, :].rearrange("p (n h) -> p n h", h=NH5), HD), ALU.mult))
                        link(v, chain, v.tensor_tensor(
                            rn[:], rn[:], over_mid(GAM[:].rearrange("p h d -> p (h d)"), NT), ALU.mult))
                        pairs = rn[:].rearrange("p n (h f two) -> p n h f two", two=2, h=NH5)
                        to = QK5.rearrange("p n (h f two) -> p n h f two", two=2, h=NH5)
                        cos = COS[:].unsqueeze(2).to_broadcast([P, NT, NH5, HD // 2])
                        sin = SIN[:].unsqueeze(2).to_broadcast([P, NT, NH5, HD // 2])
                        for part, first, second, op in ((0, cos, sin, ALU.subtract), (1, sin, cos, ALU.add)):
                            v.tensor_tensor(r1[:], pairs[:, :, :, :, 0], first, ALU.mult)
                            link(v, chain, v.tensor_tensor(r2[:], pairs[:, :, :, :, 1], second, ALU.mult))
                            link(v, chain, v.tensor_tensor(to[:, :, :, :, part], r1[:], r2[:], op))

                @block.scalar
                def _(a):
                    layernorm_scalar(a, S, NT, T)
                    for n in range(2):
                        a.wait_ge(turned.sem, turned.at(n + 1))
                        a.activation(XT[:, n * 512:(n + 1) * 512], ps[:, n, :], ACT.Copy).then_inc(copied.sem, 1)
                    if rope:
                        a.wait_ge(S("qkv_stored").sem, S("qkv_stored").at(NT))
                        a.activation(sq5[:], QKV[:, :, 0:NH5 * HD], ACT.Square).then_inc(S("rms_squared").sem, 1)
                        a.wait_ge(S("rms_sum").sem, S("rms_sum").at(1))
                        a.activation(rms[:, 2, :], rms[:, 1, :], ACT.Sqrt).then_inc(S("rms_root").sem, 1)

                @block.tensor
                def _(pe):
                    pe.wait_ge(normed.sem, normed.at(1))
                    for n in range(NT):
                        m = turn(pe, ps[:, n // 4, (n % 4) * P:(n % 4 + 1) * P], T["xn"][:, n, :], ident[:])
                        if n % 4 == 3:
                            m.then_inc(turned.sem, 1)
                    for n in range(NT):
                        pe.wait_ge(copied.sem, copied.at(n // 4 + 1))
                        if n >= 6:
                            pe.wait_ge(S("qkv_stored").sem, S("qkv_stored").at(n - 5))
                        pe.matmul(ps[:, 2 + n % 6, 0:NQKV], XT[:, n * P:(n + 1) * P], W[:], start=True,
                                  stop=True).then_inc(projected.sem, 1)
            S.close(centered=1, squared=1, var_ready=1, std_ready=1, normed=1, turned=2, turned_copied=2,
                    projected=NT, qkv_stored=NT)
            if rope:
                S.close(rms_squared=1, rms_sum=1, rms_root=1)

        with ExitStack() as c:
            K4 = sb(f"K4_{tag}", [P, NT, C], F32, c) if shared_kv else None
            ksrc = K4[:] if shared_kv else QKV[:, :, C:2 * C]
            vsrc = QKV[:, :, (H + 1) * HD:] if shared_kv else QKV[:, :, 2 * C:]
            k4_made, turned, kt_made, cleared = S("k4_made"), S("turned"), S("kt_made"), S("v2_cleared")
            with nc.Block() as block:
                @block.tensor
                def _(pe):
                    for n in range(NT):
                        m = turn(pe, ps[:, n // 4, (n % 4) * P:(n % 4 + 1) * P], QKV[:, n, 0:C], ident[:])
                        if n % 4 == 3:
                            m.then_inc(turned.sem, 1)
                    if shared_kv:
                        pe.wait_ge(k4_made.sem, k4_made.at(1))
                    for n in range(NT):
                        m = turn(pe, ps[:, 2 + n // 4, (n % 4) * P:(n % 4 + 1) * P], ksrc[:, n, :], ident[:])
                        if n % 4 == 3:
                            m.then_inc(turned.sem, 1)

                @block.vector
                def _(v):
                    v.memset(KT[:, 0:QB], 0.0)
                    if shared_kv:
                        v.tensor_copy(K4[:].rearrange("p n (h d) -> p n h d", h=H),
                                      QKV[:, :, H * HD:(H + 1) * HD].unsqueeze(2).to_broadcast([P, NT, H, HD])).then_inc(
                            k4_made.sem, 1)
                    for n in range(2):
                        v.wait_ge(turned.sem, turned.at(n + 3))
                        v.tensor_copy(KT[:, QB + n * 512:QB + (n + 1) * 512], ps[:, 2 + n, :]).then_inc(kt_made.sem, 1)
                    v.wait_ge(kt_made.sem, kt_made.at(2))
                    for h in range(H):
                        v.tensor_scalar(KE[:, h, :], KT[:], heads[:, h:h + 1], None, ALU.mult)

                @block.gpsimd
                def _(g):
                    g.memset(V2[:], 0.0).then_inc(cleared.sem, 1)

                @block.scalar
                def _(a):
                    for n in range(2):
                        a.wait_ge(turned.sem, turned.at(n + 1))
                        a.activation(QT[:, n * 512:(n + 1) * 512], ps[:, n, :], ACT.Copy)
                    a.wait_ge(cleared.sem, cleared.at(1))
                    for j in range(J):
                        src = vsrc[QB * j:QB * (j + 1)]
                        for row, blk in ((QB, j), (0, j + 1)):
                            for hh in range(HC):
                                to = V2[KB * hh + row:KB * hh + row + QB, blk:blk + (NT - 1) * J + 1:J, :]
                                if shared_kv:
                                    a.activation(to, src, ACT.Copy)
                                else:
                                    a.activation(to.rearrange("p n (c hd) -> p n c hd", c=NCH)[:, :, :, hh * HD:(hh + 1) * HD],
                                                 src.rearrange("p n (c hd) -> p n c hd", c=NCH)[:, :, :, hh * HD:(hh + 1) * HD],
                                                 ACT.Copy)
            S.close(turned=4, kt_made=2, v2_cleared=1)
            if shared_kv:
                S.close(k4_made=1)

        with ExitStack() as c:
            SH_ = sb(f"shift_{tag}", [P, 2, H * KB], F32, c)
            PR = sb(f"prob_{tag}", [P, 2, H * KB], F32, c)
            PT = sb(f"probT_{tag}", [P, 2, NCH, P], F32, c)
            MX = sb(f"max_{tag}", [P, 2, H], F32, c)
            DN = sb(f"den_{tag}", [P, 2, H], F32, c)
            RD = sb(f"rden_{tag}", [P, 2, H], F32, c)
            names = ("scored", "w_max", "w_shifted", "w_exp", "w_sum", "w_rden", "p_turned", "p_copied", "attended",
                     "o_stored")
            scored, w_max, shifted, w_exp, w_sum, w_rden, p_turned, p_copied, attended, o_stored = map(S, names)

            def scores(n):
                return ps[:, 2 * (n % 2):2 * (n % 2) + NS, :].rearrange("p s (h k) -> p (s h) k", k=KB)

            def outs(n):
                return ps[:, 6 + n % 2, 0:NCH * J * CD].rearrange("p (c j d) -> p c j d", c=NCH, j=J)

            with nc.Block() as block:
                @block.tensor
                def _(pe):
                    def score(n):
                        if n >= 2:
                            pe.wait_ge(shifted.sem, shifted.at(n - 1))
                        for s in range(NS):
                            bank = ps[:, 2 * (n % 2) + s, :].rearrange("p (h k) -> p h k", k=KB)
                            pe.matmul(bank, identb[:], over_mid(mask[:, 1 if n == 0 else 0, :], SH), start=True,
                                      stop=False, skip_group_check=True)
                            for j in range(J):
                                at = n * P + QB * j
                                m = pe.matmul(bank[QB * j:QB * (j + 1)], QT[:, at:at + QB],
                                              KE[:, s * SH:(s + 1) * SH, at:at + KB], start=False, stop=True,
                                              skip_group_check=True)
                        m.then_inc(scored.sem, 1)

                    score(0)
                    for n in range(NT):
                        if n + 1 < NT:
                            score(n + 1)
                        pe.wait_ge(w_exp.sem, w_exp.at(n + 1))
                        if n >= 1:
                            pe.wait_ge(p_copied.sem, p_copied.at(n))
                        for ch in range(NCH):
                            m = turn(pe, ps[:, 4 + ch // 4, (ch % 4) * P:(ch % 4 + 1) * P],
                                     PR[:, n % 2, ch * P:(ch + 1) * P], ident[:])
                        m.then_inc(p_turned.sem, 1)
                        pe.wait_ge(p_copied.sem, p_copied.at(n + 1))
                        if n >= 2:
                            pe.wait_ge(o_stored.sem, o_stored.at((n - 1) * J))
                        for ch in range(NCH):
                            v2 = V2[:, n * J:(n + 1) * J, :] if shared_kv else V2[:, n * J:(n + 1) * J, ch * CD:(ch + 1) * CD]
                            m = pe.matmul(outs(n)[:, ch], PT[:, n % 2, ch, :], v2, start=True, stop=True)
                        m.then_inc(attended.sem, 1)

                @block.vector
                def _(v):
                    def softmax_front(n):
                        v.wait_ge(scored.sem, scored.at(n + 1))
                        v.tensor_reduce(MX[:, n % 2, :], scores(n), AX_X, ALU.max).then_inc(w_max.sem, 1)
                        v.wait_ge(w_max.sem, w_max.at(n + 1))
                        if n >= 2:
                            v.wait_ge(w_exp.sem, w_exp.at(n - 1))
                        v.tensor_tensor(SH_[:, n % 2, :].rearrange("p (h k) -> p h k", k=KB), scores(n),
                                        over(MX[:, n % 2, :], KB), ALU.subtract).then_inc(shifted.sem, 1)

                    softmax_front(0)
                    for n in range(NT):
                        if n + 1 < NT:
                            softmax_front(n + 1)
                        v.wait_ge(w_exp.sem, w_exp.at(n + 1))
                        v.tensor_reduce(DN[:, n % 2, :], PR[:, n % 2, :].rearrange("p (h k) -> p h k", k=KB), AX_X,
                                        ALU.add).then_inc(w_sum.sem, 1)
                        v.wait_ge(w_sum.sem, w_sum.at(n + 1))
                        v.reciprocal(RD[:, n % 2, :], DN[:, n % 2, :]).then_inc(w_rden.sem, 1)
                        v.wait_ge(w_rden.sem, w_rden.at(n + 1))
                        v.wait_ge(attended.sem, attended.at(n + 1))
                        for j in range(J):
                            rows = slice(QB * j, QB * (j + 1))
                            src = outs(n)[rows, :, j, :]
                            if HC > 1:
                                src = src.rearrange("p c (h d) -> p c h d", h=HC)
                                to = AOUT[rows, n, :].rearrange("p (c h d) -> p c h d", c=NCH, h=HC)
                                rd = over(RD[rows, n % 2, :].rearrange("p (c h) -> p c h", c=NCH), HD)
                            else:
                                to = AOUT[rows, n, :].rearrange("p (c d) -> p c d", c=NCH)
                                rd = over(RD[rows, n % 2, :], HD)
                            v.tensor_tensor(to, src, rd, ALU.mult).then_inc(o_stored.sem, 1)

                @block.scalar
                def _(a):
                    def exps(n):
                        a.wait_ge(shifted.sem, shifted.at(n + 1))
                        if n >= 2:
                            a.wait_ge(p_turned.sem, p_turned.at(n - 1))
                            a.wait_ge(w_sum.sem, w_sum.at(n - 1))
                        a.activation(PR[:, n % 2, :], SH_[:, n % 2, :], ACT.Exp, scale=scale).then_inc(w_exp.sem, 1)

                    exps(0)
                    for n in range(NT):
                        if n + 1 < NT:
                            exps(n + 1)
                        a.wait_ge(p_turned.sem, p_turned.at(n + 1))
                        if n >= 2:
                            a.wait_ge(attended.sem, attended.at(n - 1))
                        a.activation(PT[:, n % 2].rearrange("p c q -> p (c q)"),
                                     ps[:, 4:6, :].rearrange("p s c -> p (s c)")[:, 0:NCH * P], ACT.Copy).then_inc(
                            p_copied.sem, 1)
            S.close(**{n: NT for n in names if n != "o_stored"}, o_stored=NT * J)

        with ExitStack() as c:
            AT = sb(f"AT_{tag}", [P, NT * P], F32, c)
            turned, copied, projected = S("turned"), S("turned_copied"), S("projected")
            with nc.Block() as block:
                @block.tensor
                def _(pe):
                    for n in range(NT):
                        m = turn(pe, ps[:, n // 4, (n % 4) * P:(n % 4 + 1) * P], AOUT[:, n, :], ident[:])
                        if n % 4 == 3:
                            m.then_inc(turned.sem, 1)
                    for n in range(NT):
                        pe.wait_ge(copied.sem, copied.at(n // 4 + 1))
                        m = pe.matmul(ps[:, 2 + n // 4, (n % 4) * P:(n % 4 + 1) * P], AT[:, n * P:(n + 1) * P], WO[:],
                                      start=True, stop=True)
                        if n % 4 == 3:
                            m.then_inc(projected.sem, 1)

                @block.scalar
                def _(a):
                    for n in range(2):
                        a.wait_ge(turned.sem, turned.at(n + 1))
                        a.activation(AT[:, n * 512:(n + 1) * 512], ps[:, n, :], ACT.Copy).then_inc(copied.sem, 1)

                @block.vector
                def _(v):
                    for n in range(2):
                        v.wait_ge(projected.sem, projected.at(n + 1))
                        xs = X[:, 4 * n:4 * n + 4, :]
                        v.tensor_tensor(xs, ps[:, 2 + n, :].rearrange("p (n c) -> p n c", n=4), xs, ALU.add)
            S.close(turned=2, turned_copied=2, projected=2)


def ffn(nc, S, ps, X, ident, WQK, WVG, WOF, H, DH, E, scale, tag):
    NT = X.shape[1]
    T = NT * P
    ED = E * DH
    HE = H * E
    NEC = ED // P
    G = 2 * NT * H
    KT = NT
    NPB = 4

    def sb(name, shape, dt=F32, c=None):
        return c.enter_context(nc.sbuf_tensor(name, shape, dt))

    with ExitStack() as ctx:
        XH = sb(f"XH_{tag}", [P, T], F32R, ctx)
        XL = sb(f"XL_{tag}", [P, T], F32R, ctx)
        PROJV = sb(f"PROJV_{tag}", [P, NT, E, DH], F32, ctx)
        MASK = sb(f"MASK_{tag}", [P, NT, 2, H, E], F32, ctx)
        MIX = sb(f"MIX_{tag}", [P, NT, H, E], F32, ctx)

        with ExitStack() as c:
            L = ln_tiles(sb, tag, NT, c)
            GT = sb(f"GT_{tag}", [P, NT, 2 * HE], F32, c)
            CNT = sb(f"CNT_{tag}", [P, G, E], BF16, c)
            GE = sb(f"GE_{tag}", [P, G, E], BF16, c)
            SG = sb(f"SG_{tag}", [P, NT, HE], F32, c)
            normed, turned, hi, lo = S("normed"), S("turned"), S("split_hi"), S("split_lo")
            valued, gated, v_stored, g_stored = S("valued"), S("gated"), S("v_stored"), S("g_stored")
            with nc.Block() as block:
                @block.tensor
                def _(pe):
                    pe.wait_ge(normed.sem, normed.at(1))
                    for n in range(NT):
                        m = turn(pe, ps[:, n // 4, (n % 4) * P:(n % 4 + 1) * P], L["xn"][:, n, :], ident[:])
                        if n % 4 == 3:
                            m.then_inc(turned.sem, 1)
                    for n in range(NT):
                        pe.wait_ge(lo.sem, lo.at(n // 4 + 1))
                        if n >= 2:
                            pe.wait_ge(v_stored.sem, v_stored.at(n - 1))
                        t = slice(n * P, (n + 1) * P)
                        parts = ((XH, 0), (XH, 1), (XL, 0))
                        for k, (xp, w) in enumerate(parts):
                            m = pe.matmul(ps[:, 2 + n % 2, :], xp[:, t], WVG[:, w, 0:ED], start=k == 0, stop=k == 2)
                        m.then_inc(valued.sem, 1)
                        for k, (xp, w) in enumerate(parts):
                            m = pe.matmul(ps[:, 4 + n // 2, 256 * (n % 2):256 * (n % 2) + 256], xp[:, t],
                                          WVG[:, w, ED:], start=k == 0, stop=k == 2)
                        m.then_inc(gated.sem, 1)

                @block.scalar
                def _(a):
                    layernorm_scalar(a, S, NT, L)
                    for n in range(2):
                        a.wait_ge(turned.sem, turned.at(n + 1))
                        a.activation(XH[:, n * 512:(n + 1) * 512], ps[:, n, :], ACT.Copy).then_inc(hi.sem, 1)
                    for n in range(NT):
                        a.wait_ge(valued.sem, valued.at(n + 1))
                        a.activation(PROJV[:, n].rearrange("p e d -> p (e d)"), ps[:, 2 + n % 2, :], ACT.Copy).then_inc(
                            v_stored.sem, 1)
                    a.wait_ge(g_stored.sem, g_stored.at(NT // 2))
                    a.activation(SG[:], GT[:, :, 0:HE], ACT.Exp, scale=-1.0).then_inc(S("g_exp").sem, 1)

                @block.vector
                def _(v):
                    chain = S("dve_chain")
                    layernorm_vector(v, S, X, L)
                    for n in range(2):
                        v.wait_ge(hi.sem, hi.at(n + 1))
                        v.tensor_tensor(XL[:, n * 512:(n + 1) * 512], ps[:, n, :],
                                        XH[:, n * 512:(n + 1) * 512].bitcast(F32), ALU.subtract).then_inc(lo.sem, 1)
                    for e in range(E):
                        v.memset(CNT[:, :, e], float(E - 1 - e)).then_inc(S("cnt_set").sem, 1)
                    for n in range(NT // 2):
                        v.wait_ge(gated.sem, gated.at(2 * n + 2))
                        v.tensor_copy(GT[:, 2 * n:2 * n + 2, :], ps[:, 4 + n, :].rearrange("p (n g) -> p n g", n=2)).then_inc(
                            g_stored.sem, 1)
                    v.wait_ge(g_stored.sem, g_stored.at(NT // 2))
                    v.wait_ge(S("cnt_set").sem, S("cnt_set").at(E))
                    g = GT[:].rearrange("p n (h e) -> p (n h) e", e=E)
                    for s in range(1, E):
                        link(v, chain, v.tensor_tensor(GE[:, :, s:E], g[:, :, 0:E - s], g[:, :, s:E], ALU.is_ge))
                        link(v, chain, v.tensor_tensor(CNT[:, :, s:E], CNT[:, :, s:E], GE[:, :, s:E], ALU.add))
                        link(v, chain, v.tensor_tensor(CNT[:, :, 0:E - s], CNT[:, :, 0:E - s], GE[:, :, s:E],
                                                       ALU.subtract))
                    link(v, chain, v.tensor_scalar(MASK[:].rearrange("p n k h e -> p (n k h) e"), CNT[:], 2.0, None,
                                                   ALU.is_lt))
                    v.wait_ge(S("g_exp").sem, S("g_exp").at(1))
                    link(v, chain, v.tensor_scalar(SG[:], SG[:], 1.0, None, ALU.add))
                    link(v, chain, v.reciprocal(SG[:], SG[:]))
                    v.tensor_tensor(MIX[:].rearrange("p n h e -> p n (h e)"), SG[:],
                                    MASK[:, :, 0].rearrange("p n h e -> p n (h e)"), ALU.mult)
            S.close(centered=1, squared=1, var_ready=1, std_ready=1, normed=1, turned=2, split_hi=2, split_lo=2,
                    valued=NT, gated=NT, v_stored=NT, g_stored=NT // 2, cnt_set=E, g_exp=1)

        with ExitStack() as c2:
            A = sb(f"A_{tag}", [P, NT, E, DH], F32, c2)
            with ExitStack() as c:
                WS = [sb(f"WS{i}_{tag}", [P, 2, 2 * DH], F32R, c) for i in range(2)]
                QH = [sb(f"QH{i}_{tag}", [P, T], F32R, c) for i in range(2)]
                QL = [sb(f"QL{i}_{tag}", [P, T], F32R, c) for i in range(2)]
                KHL = [sb(f"KHL{i}_{tag}", [P, T], F32R, c) for i in range(2)]
                KH1 = [sb(f"KH1{i}_{tag}", [P, T], F32R, c) for i in range(2)]
                NH = [sb(f"NH{i}_{tag}", [P, NT, 2], F32, c) for i in range(2)]
                NM = [sb(f"NM{i}_{tag}", [P, NT], F32, c) for i in range(2)]
                ROW = [sb(f"ROW{i}_{tag}", [NT, P], F32R, c) for i in range(2)]
                PB = [sb(f"PB{i}_{tag}", [P, T], F32, c) for i in range(NPB)]
                V1 = [sb(f"V1{i}_{tag}", [P, KT, DH + 1], F32, c) for i in range(2)]
                VT = [sb(f"VT{i}_{tag}", [P, KT, DH], F32, c) for i in range(2)]
                OS = [sb(f"OS{i}_{tag}", [P, NT, DH + 1], F32, c) for i in range(2)]
                RDN = sb(f"RDN_{tag}", [P, NT], F32, c)
                MW = sb(f"MW_{tag}", [P, NT, E], F32, c)
                OP = [sb(f"OP{i}_{tag}", [P, E, DH], F32, c) for i in range(2)]

                staged, consts = [S("w_staged0"), S("w_staged1")], S("head_consts")
                m_filled, m_freed = S("m_filled"), S("m_freed")
                qk_hi, kh1 = S("qk_hi"), S("kh1_ready")
                max_ready = S("max_ready")
                row_made, row_set = S("row_made"), S("row_set")
                s_filled, exped, p_freed = S("s_filled"), S("exped"), S("p_freed")
                o_evac, v_step = S("o_evac"), S("v_step")
                o_rden, o_weight, o_prod, o_added = S("o_rden"), S("o_weight"), S("o_prod"), S("o_added")
                R = 2 * NT + 2
                HALVES = {0: 2, 1: 3, 2: 4, 3: 3, 4: 4}
                VS = 2 * E - 1
                M = ps[:, 0:2, :]
                M1 = M.rearrange("p s c -> p (s c)")
                Sb = [ps[:, 2:4, :], ps[:, 4:6, :]]

                def O(t):
                    return ps[:, 6 + t // 4, (t % 4) * (DH + 1):(t % 4 + 1) * (DH + 1)]

                with nc.Block() as block:
                    @block.sync
                    def _(sp):
                        def stage(h, p):
                            sp.dma_start(WS[p][:].rearrange("c o d -> c (o d)").bitcast(F32),
                                         WQK[:, bass.ds(h, 1)].rearrange("c o k d -> c (o k d)").bitcast(F32)).then_inc(staged[p].sem, 16)

                        def row(h, p):
                            sp.wait_ge(row_made.sem, row_made.at(h + 1))
                            sp.dma_start(QL[p][DH:DH + 1, :].bitcast(F32).rearrange("o (t q) -> o t q", t=NT),
                                         ROW[p][:].bitcast(F32)).then_inc(row_set.sem, 16)

                        stage(0, 0)
                        stage(1, 1)
                        sp.wait_ge(consts.sem, consts.at(4))
                        row(0, 0)

                        def body(h, p):
                            sp.wait_ge(m_filled.sem, m_filled.at(R * h + 1))
                            stage(h + 2, p)
                            row(h + 1, 1 - p)

                        with sp.Fori(0, H // 2 - 1) as i:
                            body(2 * i, 0)
                            body(2 * i + 1, 1)
                        row(H - 1, 1)

                    @block.gpsimd
                    def _(g):
                        for i in range(2):
                            g.memset(V1[i][:, :, DH:DH + 1], 1.0)

                        def mix(h, p):
                            weight = MIX[:, :, bass.ds(h, 1), :].rearrange("p n o e -> p n (o e)")
                            to = V1[p][:, :, 0:DH]
                            g.tensor_tensor(to, PROJV[:, :, 0, :], over(weight[:, :, 0], DH), ALU.mult).then_inc(
                                v_step.sem, 1)
                            g.wait_ge(v_step.sem, v_step.at(VS * h))
                            for e in range(1, E):
                                g.tensor_tensor(VT[e % 2][:], PROJV[:, :, e, :], over(weight[:, :, e], DH),
                                                ALU.mult).then_inc(v_step.sem, 1)
                                g.wait_ge(v_step.sem, v_step.at(VS * h + 2 * e))
                                g.tensor_tensor(to, to, VT[e % 2][:], ALU.add).then_inc(v_step.sem, 1)

                        mix(0, 0)
                        mix(1, 1)

                        def body(h, p):
                            g.wait_ge(p_freed.sem, p_freed.at(NPB + KT * (h + 1)))
                            mix(h + 2, p)

                        with g.Fori(0, H // 2 - 1) as i:
                            body(2 * i, 0)
                            body(2 * i + 1, 1)

                    @block.tensor
                    def _(pe):
                        def project(h, p):
                            if not (isinstance(h, int) and h == 0):
                                pe.wait_ge(m_freed.sem, m_freed.at(R * h))
                            pe.wait_ge(staged[p].sem, staged[p].at(8 * (h - p) + 16))
                            for k, (w, xp) in enumerate(((0, XH), (0, XL), (1, XH))):
                                for half in range(2):
                                    m = pe.matmul(M[:, half, :], WS[p][:, w, :], xp[:, half * 512:(half + 1) * 512],
                                                  start=k == 0, stop=k == 2)
                            m.then_inc(m_filled.sem, 1)

                        def max_scores(h, p, i):
                            pe.wait_ge(m_freed.sem, m_freed.at(R * h + max(i, 1)))
                            pe.matmul(M[:, i % 2, :], QH[p][:, (i // 2) * P:(i // 2 + 1) * P],
                                      KHL[p][:, (i % 2) * 512:(i % 2 + 1) * 512], start=True, stop=True).then_inc(
                                m_filled.sem, 1)

                        def max_turn(h, p):
                            pe.wait_ge(max_ready.sem, max_ready.at(h + 1))
                            turn(pe, M[0:NT, 0, 0:P], NM[p][:], ident[:]).then_inc(m_filled.sem, 1)

                        def scores(h, p, k):
                            n = KT * h + k
                            pe.wait_ge(exped.sem, exped.at(n + 1))
                            if k == 0:
                                pe.wait_ge(row_set.sem, row_set.at(16 * (h + 1)))
                                pe.wait_ge(kh1.sem, kh1.at(h + 1))
                            keys = slice(k * P, (k + 1) * P)
                            for half in range(2):
                                pe.matmul(Sb[k % 2][:, half, :], KHL[p][:, keys], QH[p][:, half * 512:(half + 1) * 512],
                                          start=True, stop=False)
                            for half in range(2):
                                m = pe.matmul(Sb[k % 2][:, half, :], KH1[p][:, keys],
                                              QL[p][:, half * 512:(half + 1) * 512], start=False, stop=True)
                            m.then_inc(s_filled.sem, 1)

                        def attend(p, k, tiles):
                            for t in tiles:
                                m = pe.matmul(O(t), PB[k % NPB][:, t * P:(t + 1) * P], V1[p][:, k, :],
                                              start=(k == 0 and t % 4 == 0), stop=(k == KT - 1), skip_group_check=True)
                            return m

                        def body(h, p, more=True, project_next=True):
                            i = 0
                            for k in range(KT):
                                if k + 1 < KT:
                                    scores(h, p, k + 1)
                                elif more:
                                    scores(h + 1, 1 - p, 0)
                                if project_next and k == KT - 2:
                                    project(h + 2, p)
                                pe.wait_ge(exped.sem, exped.at(2 + KT * h + k + 1))
                                if k == 0:
                                    pe.wait_ge(v_step.sem, v_step.at(VS * (h + 1)))
                                    pe.wait_ge(o_evac.sem, o_evac.at(h + 1))
                                for part in range(4):
                                    m = attend(p, k, range(2 * part, 2 * part + 2))
                                    if part == 3:
                                        m.then_inc(p_freed.sem, 1)
                                    if more and part >= 4 - HALVES.get(k, 0):
                                        max_scores(h + 1, 1 - p, i)
                                        i += 1
                                    if more and k == 5 and part == 2:
                                        max_turn(h + 1, 1 - p)

                        pe.sem_inc(p_freed.sem, NPB)
                        pe.wait_ge(consts.sem, consts.at(4))
                        project(0, 0)
                        for i in range(2 * NT):
                            max_scores(0, 0, i)
                        max_turn(0, 0)
                        project(1, 1)
                        scores(0, 0, 0)
                        with pe.Fori(0, H // 2 - 1) as i:
                            body(2 * i, 0)
                            body(2 * i + 1, 1)
                        body(H - 2, 0, project_next=False)
                        body(H - 1, 1, more=False, project_next=False)

                    @block.scalar
                    def _(a):
                        def q_high(h, p):
                            a.wait_ge(m_filled.sem, m_filled.at(R * h + 1))
                            a.activation(QH[p][0:DH, :], M1[0:DH], ACT.Copy, scale=scale)
                            a.activation(QH[p][DH:2 * DH, :], M1[0:DH], ACT.Copy, scale=scale)

                        def k_high(p):
                            a.activation(KHL[p][0:DH, :], M1[DH:2 * DH], ACT.Copy).then_inc(qk_hi.sem, 1)

                        def k_high_again(h, p):
                            a.wait_ge(qk_hi.sem, qk_hi.at(h + 1))
                            a.activation(KH1[p][0:DH, :], KHL[p][0:DH, :].bitcast(F32), ACT.Copy).then_inc(kh1.sem, 1)

                        def row(h, p, reused=True):
                            a.wait_ge(m_filled.sem, m_filled.at(R * (h + 1)))
                            if reused:
                                a.wait_ge(row_set.sem, row_set.at(16 * h))
                            a.activation(ROW[p][:], M[0:NT, 0, 0:P], ACT.Copy).then_inc(row_made.sem, 1)
                            a.wait_ge(row_made.sem, row_made.at(h + 1))
                            a.sem_inc(m_freed.sem, 1)

                        def exp(h, k):
                            a.wait_ge(s_filled.sem, s_filled.at(KT * h + k + 1))
                            a.wait_ge(p_freed.sem, p_freed.at(KT * h + k + 1))
                            a.activation(PB[k % NPB][:], Sb[k % 2].rearrange("p s c -> p (s c)"), ACT.Exp).then_inc(
                                exped.sem, 1)

                        def evacuate(h, p):
                            a.wait_ge(p_freed.sem, p_freed.at(NPB + KT * (h + 1)))
                            a.wait_ge(o_added.sem, o_added.at(NT * (h + 1)))
                            for half in range(2):
                                m = a.activation(OS[p][:, 4 * half:4 * half + 4, :].rearrange("p t d -> p (t d)"),
                                                 ps[:, 6 + half, 0:4 * (DH + 1)], ACT.Copy)
                            m.then_inc(o_evac.sem, 1)

                        def body(h, p, more=True, project_next=True):
                            exp(h, 1)
                            exp(h, 2)
                            if more:
                                k_high_again(h + 1, 1 - p)
                            for k in range(3, KT):
                                exp(h, k)
                                if more and k == KT - 2:
                                    row(h + 1, 1 - p)
                            if project_next:
                                q_high(h + 2, p)
                                k_high(p)
                            if more:
                                exp(h + 1, 0)
                            evacuate(h, p)

                        a.sem_inc(exped.sem, 2)
                        a.sem_inc(o_evac.sem, 1)
                        a.wait_ge(consts.sem, consts.at(4))
                        q_high(0, 0)
                        k_high(0)
                        k_high_again(0, 0)
                        row(0, 0, reused=False)
                        q_high(1, 1)
                        k_high(1)
                        exp(0, 0)
                        with a.Fori(0, H // 2 - 1) as i:
                            body(2 * i, 0)
                            body(2 * i + 1, 1)
                        body(H - 2, 0, project_next=False)
                        body(H - 1, 1, more=False, project_next=False)

                    @block.vector
                    def _(v):
                        for i in range(2):
                            v.memset(KH1[i][DH:, :].bitcast(F32), 0.0)
                            v.memset(QL[i][DH:, :].bitcast(F32), 0.0).then_inc(consts.sem, 1)
                        v.wait_ge(consts.sem, consts.at(2))
                        v.memset(A[:], 0.0)
                        for i in range(2):
                            v.memset(KH1[i][DH:DH + 1, :].bitcast(F32), 1.0).then_inc(consts.sem, 1)
                        v.sem_inc(o_added.sem, 2 * NT)

                        def low(h, p):
                            v.wait_ge(qk_hi.sem, qk_hi.at(h + 1))
                            v.scalar_tensor_tensor(QL[p][0:DH, :], M1[0:DH], scale, QH[p][0:DH, :].bitcast(F32),
                                                   ALU.mult, ALU.subtract)
                            v.tensor_tensor(KHL[p][DH:2 * DH, :], M1[DH:2 * DH], KHL[p][0:DH, :].bitcast(F32),
                                            ALU.subtract).then_inc(m_freed.sem, 1)

                        def maximum(h, p, i):
                            v.wait_ge(m_filled.sem, m_filled.at(R * h + 2 + i))
                            v.tensor_reduce(NH[p][:, i // 2, i % 2:i % 2 + 1], M[:, i % 2, :], AX_X,
                                            ALU.max).then_inc(m_freed.sem, 1)

                        def maxima(h, p):
                            v.wait_ge(m_freed.sem, m_freed.at(R * h + 1 + 2 * NT))
                            v.tensor_reduce(NM[p][:], NH[p][:], AX_X, ALU.max, negate=True).then_inc(max_ready.sem, 1)

                        def weights(h, p):
                            v.wait_ge(o_evac.sem, o_evac.at(h + 2))
                            v.reciprocal(RDN[:], OS[p][:, :, DH]).then_inc(o_rden.sem, 1)
                            v.wait_ge(o_rden.sem, o_rden.at(h + 1))
                            gate = MASK[:, :, 1, bass.ds(h, 1), :].rearrange("p n o e -> p n (o e)")
                            v.tensor_tensor(MW[:], gate, over(RDN[:], E), ALU.mult).then_inc(o_weight.sem, 1)
                            v.wait_ge(o_weight.sem, o_weight.at(h + 1))

                        def product(h, p, t):
                            v.wait_ge(o_added.sem, o_added.at(NT * (h + 2) + t - 1))
                            v.tensor_tensor(OP[t % 2][:], over_mid(OS[p][:, t, 0:DH], E), over(MW[:, t, :], DH),
                                            ALU.mult).then_inc(o_prod.sem, 1)

                        def added(h, t):
                            v.wait_ge(o_prod.sem, o_prod.at(NT * h + t + 1))
                            v.tensor_tensor(A[:, t], A[:, t], OP[t % 2][:], ALU.add).then_inc(o_added.sem, 1)

                        def sum_steps(h, p):
                            yield lambda: product(h, p, 0)
                            for t in range(NT):
                                if t + 1 < NT:
                                    yield lambda t=t: product(h, p, t + 1)
                                yield lambda t=t: added(h, t)

                        def body(h, p):
                            low(h + 1, 1 - p)
                            maximum(h + 1, 1 - p, 0)
                            maximum(h + 1, 1 - p, 1)
                            weights(h - 1, 1 - p)
                            steps = sum_steps(h - 1, 1 - p)
                            for i in range(2, 2 * NT):
                                if i % 2 == 0:
                                    next(steps)()
                                maximum(h + 1, 1 - p, i)
                            maxima(h + 1, 1 - p)
                            for step in steps:
                                step()

                        for h in range(2):
                            low(h, h)
                            for i in range(2 * NT):
                                maximum(h, h, i)
                            maxima(h, h)
                        with v.Fori(0, H // 2 - 1) as i:
                            body(2 * i + 1, 1)
                            body(2 * i + 2, 0)
                        for h in range(H - 2, H):
                            weights(h, h % 2)
                            for step in sum_steps(h, h % 2):
                                step()
                S.close(w_staged0=8 * H, w_staged1=8 * H, head_consts=4, m_filled=R * H, m_freed=R * H, qk_hi=H, kh1_ready=H,
                        row_made=H, max_ready=H, row_set=16 * H, s_filled=KT * H, exped=2 + KT * H, p_freed=NPB + KT * H, o_evac=H + 1,
                        v_step=VS * H, o_rden=H, o_weight=H, o_prod=NT * H, o_added=NT * (H + 2))

            with ExitStack() as c:
                AT = sb(f"AT_{tag}", [P, NEC, T], F32, c)
                turned, copied, projected = S("turned"), S("turned_copied"), S("projected")
                with nc.Block() as block:
                    @block.tensor
                    def _(pe):
                        for n in range(NT):
                            if n >= 4:
                                pe.wait_ge(copied.sem, copied.at(n - 3))
                            for ec in range(NEC):
                                m = turn(pe, ps[:, n % 4, ec * P:(ec + 1) * P],
                                         A[:, n].rearrange("p e d -> p (e d)")[:, ec * P:(ec + 1) * P], ident[:])
                            m.then_inc(turned.sem, 1)
                        for n in range(NT):
                            pe.wait_ge(copied.sem, copied.at(n + 1))
                            for ec in range(NEC):
                                m = pe.matmul(ps[:, 4 + n // 4, (n % 4) * P:(n % 4 + 1) * P], AT[:, ec, n * P:(n + 1) * P],
                                              WOF[:, ec, :], start=ec == 0, stop=ec == NEC - 1)
                            if n % 4 == 3:
                                m.then_inc(projected.sem, 1)

                    @block.scalar
                    def _(a):
                        for n in range(NT):
                            a.wait_ge(turned.sem, turned.at(n + 1))
                            a.activation(AT[:, :, n * P:(n + 1) * P], ps[:, n % 4, :].rearrange("p (e q) -> p e q", e=NEC),
                                         ACT.Copy).then_inc(copied.sem, 1)

                    @block.vector
                    def _(v):
                        for n in range(2):
                            v.wait_ge(projected.sem, projected.at(n + 1))
                            xs = X[:, 4 * n:4 * n + 4, :]
                            v.tensor_tensor(xs, ps[:, 4 + n, :].rearrange("p (n c) -> p n c", n=4), xs, ALU.add)
                S.close(turned=NT, turned_copied=NT, projected=2)


_INS = ["L0_attn_a_x", "L0_attn_a_Wq", "L0_attn_a_Wk", "L0_attn_a_Wv", "L0_attn_a_Wo", "L0_attn_a_q_gamma",
        "L0_attn_a_k_gamma", "L0_attn_b_wq", "L0_attn_b_wk", "L0_attn_b_wv", "L0_attn_b_wo", "L0_ffn_Wq",
        "L0_ffn_Wk", "L0_ffn_Wv", "L0_ffn_Ws", "L0_ffn_Wd", "L0_ffn_Wo"]


def rope_tables(T, head_dim):
    exponent = np.arange(0, head_dim, 2, dtype=np.float32) / np.float32(head_dim)
    inv_freq = (np.float32(1.0) / np.power(np.float32(1000000.0), exponent)).astype(np.float32)
    angles = np.outer(np.arange(T, dtype=np.float32), inv_freq).astype(np.float32)
    return np.cos(angles.astype(np.float64)).astype(np.float32), np.sin(angles.astype(np.float64)).astype(np.float32)


def kernel(**inputs):
    import concourse.bacc as _bacc
    from concourse.bass_utils import run_bass_kernel_spmd as _run

    nc = _bacc.Bacc("TRN2", target_bir_lowering=False, num_devices=1)
    arrays, args = {}, {}
    for name in _INS:
        a = np.ascontiguousarray(inputs[name])
        arrays[f"in_{name}_dram"] = a
        args[name] = nc.dram_tensor(f"in_{name}_dram", a.shape, mybir.dt.from_np(a.dtype), kind="ExternalInput").ap()
    shape = args["L0_attn_a_x"].shape
    cos, sin = rope_tables(shape[1], 32)
    for name, a in (("rope_cos", cos), ("rope_sin", sin)):
        arrays[f"in_{name}_dram"] = a
        args[name] = nc.dram_tensor(f"in_{name}_dram", a.shape, mybir.dt.from_np(a.dtype), kind="ExternalInput").ap()
    out = nc.dram_tensor("out_0_dram", shape, F32, kind="ExternalOutput").ap()
    build(nc, args, out)
    r = _run(nc, [arrays], core_ids=[0])
    return r.results[0]["out_0_dram"]
```

```python
from contextlib import ExitStack
from itertools import islice

import numpy as np

import concourse.bass as bass
from concourse import mybir

ALU = mybir.AluOpType
ACT = mybir.ActivationFunctionType
AX_X = mybir.AxisListType.X
F32 = mybir.dt.float32
F32R = mybir.dt.float32r
BF16 = mybir.dt.bfloat16

P = 128
C = 128
LN_EPS = 1e-5
RMS_EPS = 1e-6
NEG = -1e30


class Signal:

    def __init__(self, ctx, nc, name):
        self.sem = ctx.enter_context(nc.semaphore(name))
        self.base = 0

    def at(self, k):
        return self.base + k


class Signals:

    def __init__(self, ctx, nc):
        self.ctx, self.nc, self.all = ctx, nc, {}

    def __call__(self, name):
        if name not in self.all:
            self.all[name] = Signal(self.ctx, self.nc, name)
        return self.all[name]

    def close(self, **made):
        for name, n in made.items():
            self.all[name].base += n


def link(eng, sig, ins):
    ins.then_inc(sig.sem, 1)
    sig.base += 1
    eng.wait_ge(sig.sem, sig.base)


def over(ap, n):
    return ap.unsqueeze(len(ap.shape)).to_broadcast(list(ap.shape) + [n])


def over_mid(ap, n):
    return ap.unsqueeze(1).to_broadcast([ap.shape[0], n] + list(ap.shape[1:]))


def turn(pe, out, block, ident):
    return pe.matmul(out, block, ident, start=True, stop=True)


def layernorm_vector(v, S, X, T):
    chain = S("dve_chain")
    NT = X.shape[1]
    for n in range(NT):
        m = v.bn_stats(T["stats"][:, n, :], X[:, n, :])
    link(v, chain, m)
    for n in range(NT):
        m = v.bn_aggr(T["mean_var"][:, n, :], T["stats"][:, n, :])
    link(v, chain, m)
    v.tensor_scalar(T["var"][:], T["mean_var"][:, :, 1], LN_EPS, None, ALU.add).then_inc(S("var_ready").sem, 1)
    v.wait_ge(S("std_ready").sem, S("std_ready").at(1))
    link(v, chain, v.reciprocal(T["rstd"][:], T["std"][:]))
    for n in range(NT):
        m = v.tensor_scalar(T["xn"][:, n, :], X[:, n, :], T["mean_var"][:, n, 0:1], T["rstd"][:, n:n + 1],
                            ALU.subtract, ALU.mult)
        if n % (NT // 2) == NT // 2 - 1:
            m.then_inc(S("normed").sem, 1)


def layernorm_scalar(a, S, T, ident):
    a.activation(T["warm"][:], ident[:, 0:1], ACT.Sqrt)
    a.wait_ge(S("var_ready").sem, S("var_ready").at(1))
    a.activation(T["std"][:], T["var"][:], ACT.Sqrt).then_inc(S("std_ready").sem, 1)


def build(nc, IN, out):
    x_in = IN["L0_attn_a_x"]
    B, T, _ = x_in.shape
    NT = T // P
    HF, DH, _ = IN["L0_ffn_Wq"].shape
    E = IN["L0_ffn_Wv"].shape[0]
    ED = E * DH
    NEC = ED // P
    HE = HF * E
    FFN_SCALE = float(DH) ** -0.5

    with ExitStack() as ctx:
        def sb(name, shape, dt=F32, c=ctx):
            return c.enter_context(nc.sbuf_tensor(name, shape, dt))

        S = Signals(ctx, nc)
        ps = ctx.enter_context(nc.psum_tensor("ps", [P, 8, 512], F32))

        X = sb("X", [P, B * NT, C])
        ident = sb("ident", [P, P])
        identb = sb("identb", [P, P], BF16)
        later = sb("later", [P, E], BF16)
        WQK = sb("WQK", [P, HF, 2, 2 * DH], F32R)
        WVG = sb("WVG", [P, 2, ED + 2 * HE], F32R)
        WOF = sb("WOF", [P, NEC, C])
        GAM = sb("GAM", [P, 5, 32])
        COS = sb("COS", [P, NT, 16])
        SIN = sb("SIN", [P, NT, 16])

        A_H, A_HD, A_QB, A_LO = 4, 32, 64, 0
        B_H, B_HD, B_QB, B_LO = 16, 8, 32, 1
        WA = sb("WA", [P, 192])
        WOA = sb("WOA", [P, C])
        WB = sb("WB", [P, 3 * C])
        WOB = sb("WOB", [P, C])
        masks = {"a": sb("mask_a", [P, 2, 2 * A_QB], BF16), "b": sb("mask_b", [P, 2, 2 * B_QB], BF16)}
        heads = {"a": sb("heads_a", [P, A_H]), "b": sb("heads_b", [P, B_H])}

        with ExitStack() as c:
            raw = sb("raw", [P, 30, C], F32, c)
            Q0, K0, V0, S0, D0, O0, AQ, AKV, AO, BQ = 0, 8, 16, 20, 21, 22, 26, 27, 28, 29
            rawb = sb("rawb", [P, 3, C], F32, c)
            loads = []

            def load(dst, src):
                loads.append((dst, src))

            load(X[:, 0:NT, :], x_in[0].rearrange("(n p) c -> p n c", p=P))
            load(raw[:, Q0:Q0 + 8, :], IN["L0_ffn_Wq"].rearrange("h d c -> (h d) c").rearrange("(n p) c -> p n c", p=P))
            load(raw[:, K0:K0 + 8, :], IN["L0_ffn_Wk"].rearrange("h d c -> (h d) c").rearrange("(n p) c -> p n c", p=P))
            load(raw[:, V0:V0 + 4, :], IN["L0_ffn_Wv"].rearrange("h d c -> (h d) c").rearrange("(n p) c -> p n c", p=P))
            load(raw[:, S0, :], IN["L0_ffn_Ws"].rearrange("h e c -> (h e) c"))
            load(raw[:, D0, :], IN["L0_ffn_Wd"].rearrange("h e c -> (h e) c"))
            load(raw[:, O0:O0 + 4, :].rearrange("f n (e d) -> f (n e) d", d=DH), IN["L0_ffn_Wo"].rearrange("e f d -> f e d"))
            load(raw[:, AQ, :], IN["L0_attn_a_Wq"])
            load(raw[0:32, AKV, :], IN["L0_attn_a_Wk"])
            load(raw[32:64, AKV, :], IN["L0_attn_a_Wv"])
            load(raw[:, AO, :], IN["L0_attn_a_Wo"])
            load(raw[:, BQ, :], IN["L0_attn_b_wq"])
            load(rawb[:, 0, :], IN["L0_attn_b_wk"])
            load(rawb[:, 1, :], IN["L0_attn_b_wv"])
            load(rawb[:, 2, :], IN["L0_attn_b_wo"])
            for n in range(4):
                load(GAM[:, n, :], IN["L0_attn_a_q_gamma"].rearrange("(a d) -> a d", a=1).to_broadcast([P, 32]))
            load(GAM[:, 4, :], IN["L0_attn_a_k_gamma"].rearrange("(a d) -> a d", a=1).to_broadcast([P, 32]))
            load(COS[:], IN["rope_cos"].rearrange("(n p) f -> p n f", p=P))
            load(SIN[:], IN["rope_sin"].rearrange("(n p) f -> p n f", p=P))
            load(X[:, NT:2 * NT, :], x_in[1].rearrange("(n p) c -> p n c", p=P))
            n_loads = len(loads)
            loaded, made, turned, split, moved = S("loaded"), S("const_made"), S("turned"), S("split_hi"), S("bank_freed")

            with nc.Block() as block:
                @block.sync
                def _(sp):
                    for dst, src in loads[0::2]:
                        sp.dma_start(dst, src).then_inc(loaded.sem, 16)

                @block.gpsimd
                def _(g):
                    chain = S("pool_chain")
                    link(g, chain, g.memset(ident[:], 0.0))
                    link(g, chain, g.affine_select(out=ident[:], in_=ident[:], compare_op=ALU.not_equal, fill=1.0,
                                                   base=0, pattern=[[-1, P]], channel_multiplier=1))
                    g.tensor_copy(identb[:], ident[:]).then_inc(made.sem, 1)
                    for key, QB, H, HD, LO in (("a", A_QB, A_H, A_HD, A_LO), ("b", B_QB, B_H, B_HD, B_LO)):
                        m, KB = masks[key], 2 * QB
                        link(g, chain, g.memset(m[:], 0.0))
                        for j in range(P // QB):
                            v = m[QB * j:QB * (j + 1), :, :]
                            link(g, chain, g.affine_select(out=v, in_=v, compare_op=ALU.is_ge, fill=NEG, base=-LO,
                                                           pattern=[[0, 2], [1, KB]], channel_multiplier=-1))
                            link(g, chain, g.affine_select(out=v, in_=v, compare_op=ALU.is_ge, fill=NEG, base=QB,
                                                           pattern=[[0, 2], [-1, KB]], channel_multiplier=1))
                        v = m[0:QB, 1, :]
                        link(g, chain, g.affine_select(out=v, in_=v, compare_op=ALU.is_ge, fill=NEG, base=-QB,
                                                       pattern=[[1, KB]], channel_multiplier=0))
                        h = heads[key]
                        link(g, chain, g.memset(h[:], 1.0))
                        link(g, chain, g.affine_select(out=h[:], in_=h[:], compare_op=ALU.is_ge, fill=0.0, base=0,
                                                       pattern=[[-HD, H]], channel_multiplier=1))
                        link(g, chain, g.affine_select(out=h[:], in_=h[:], compare_op=ALU.is_ge, fill=0.0, base=HD - 1,
                                                       pattern=[[HD, H]], channel_multiplier=-1))
                    for e in range(E):
                        link(g, chain, g.memset(later[:, e:e + 1], float(E - 1 - e)))

                banks = [[(Q0 + n) for n in range(4)], [(Q0 + 4 + n) for n in range(4)],
                         [(K0 + n) for n in range(4)], [(K0 + 4 + n) for n in range(4)],
                         [(V0 + n) for n in range(4)], [S0, D0, AQ, AO], [(O0 + n) for n in range(4)],
                         [BQ, "wk", "wv", "wo"]]

                @block.tensor
                def _(pe):
                    pe.wait_ge(loaded.sem, loaded.at(16 * n_loads))
                    pe.wait_ge(made.sem, made.at(1))
                    for b, blocks in enumerate(banks):
                        for n, r in enumerate(blocks):
                            src = rawb[:, ("wk", "wv", "wo").index(r), :] if isinstance(r, str) else raw[:, r, :]
                            m = turn(pe, ps[:, b, n * P:(n + 1) * P], src, ident[:])
                        m.then_inc(turned.sem, 1)
                    pe.wait_ge(moved.sem, moved.at(1))
                    turn(pe, ps[:, 0, 0:64], raw[0:64, AKV, :], ident[0:64, 0:64]).then_inc(turned.sem, 1)

                @block.scalar
                def _(a):
                    for dst, src in loads[1::2]:
                        a.dma_start(dst, src).then_inc(loaded.sem, 16)
                    for b in range(4):
                        a.wait_ge(turned.sem, turned.at(b + 1))
                        dst = WQK[:, 8 * (b % 2):8 * (b % 2) + 8, 0, DH * (b // 2):DH * (b // 2) + DH]
                        a.activation(dst, ps[:, b, :].rearrange("c (h d) -> c h d", d=DH), ACT.Copy).then_inc(split.sem, 1)
                    a.wait_ge(turned.sem, turned.at(5))
                    a.activation(WVG[:, 0, 0:ED], ps[:, 4, :], ACT.Copy).then_inc(split.sem, 1)
                    a.wait_ge(turned.sem, turned.at(6))
                    a.activation(WVG[:, 0, ED:], ps[:, 5, 0:2 * HE], ACT.Copy).then_inc(split.sem, 1)

                @block.vector
                def _(v):
                    for b in range(4):
                        v.wait_ge(split.sem, split.at(b + 1))
                        hi = WQK[:, 8 * (b % 2):8 * (b % 2) + 8, 0, DH * (b // 2):DH * (b // 2) + DH]
                        lo = WQK[:, 8 * (b % 2):8 * (b % 2) + 8, 1, DH * (b // 2):DH * (b // 2) + DH]
                        d = v.tensor_tensor(lo, ps[:, b, :].rearrange("c (h d) -> c h d", d=DH), hi.bitcast(F32), ALU.subtract)
                        if b == 0:
                            d.then_inc(moved.sem, 1)
                    v.wait_ge(split.sem, split.at(5))
                    v.tensor_tensor(WVG[:, 1, 0:ED], ps[:, 4, :], WVG[:, 0, 0:ED].bitcast(F32), ALU.subtract)
                    v.wait_ge(split.sem, split.at(6))
                    v.tensor_tensor(WVG[:, 1, ED:], ps[:, 5, 0:2 * HE], WVG[:, 0, ED:].bitcast(F32), ALU.subtract)
                    v.tensor_copy(WA[:, 0:C], ps[:, 5, 2 * P:3 * P])
                    v.tensor_copy(WOA[:], ps[:, 5, 3 * P:4 * P])
                    v.wait_ge(turned.sem, turned.at(7))
                    v.tensor_copy(WOF[:], ps[:, 6, :].rearrange("p (n f) -> p n f", n=NEC))
                    v.wait_ge(turned.sem, turned.at(8))
                    v.tensor_copy(WB[:], ps[:, 7, 0:3 * P])
                    v.tensor_copy(WOB[:], ps[:, 7, 3 * P:4 * P])
                    v.wait_ge(turned.sem, turned.at(9))
                    v.tensor_copy(WA[:, C:C + 64], ps[:, 0, 0:64])
            S.close(loaded=16 * n_loads, const_made=1, turned=9, split_hi=6, bank_freed=1)

        for b in range(B):
            Xb = X[:, b * NT:(b + 1) * NT, :]
            windowed(nc, S, ps, Xb, ident, identb, WA, WOA, masks["a"], heads["a"], H=A_H, HD=A_HD, QB=A_QB,
                     tag=f"a{b}", rope=(GAM, COS, SIN))
            ffn(nc, S, ps, Xb, ident, later, WQK, WVG, WOF, HF, DH, E, FFN_SCALE, tag=f"f{b}")
            windowed(nc, S, ps, Xb, ident, identb, WB, WOB, masks["b"], heads["b"], H=B_H, HD=B_HD, QB=B_QB,
                     tag=f"b{b}", rope=None)
            ffn(nc, S, ps, Xb, ident, later, WQK, WVG, WOF, HF, DH, E, FFN_SCALE, tag=f"g{b}")
            with nc.Block() as block:
                @block.sync
                def _(sp):
                    sp.dma_start(out[b].rearrange("(n p) c -> p n c", p=P), Xb).then_inc(S("stored").sem, 16)
                    sp.wait_ge(S("stored").sem, S("stored").at(16))
            S.close(stored=16)


def ln_tiles(sb, NT, xn):
    shapes = dict(stats=[P, NT, 6], mean_var=[P, NT, 2], var=[P, NT], std=[P, NT], rstd=[P, NT], warm=[P, 1])
    return {"xn": xn} | {n: sb(n, shape) for n, shape in shapes.items()}


def windowed(nc, S, ps, X, ident, identb, W, WO, mask, heads, H, HD, QB, tag, rope):
    NT = X.shape[1]
    J = P // QB
    KB = 2 * QB
    HC = P // KB
    NCH = H // HC
    CD = HC * HD
    NB = NT * J
    shared_kv = rope is not None
    NQKV = W.shape[1]
    scale = float(HD) ** -0.5
    SH = 512 // KB
    NS = H // SH
    VW = HD if shared_kv else C

    def sb(name, shape, dt=F32, c=None):
        return c.enter_context(nc.sbuf_tensor(name, shape, dt))

    with ExitStack() as ctx:
        QKV = sb(f"QKV_{tag}", [P, NT, NQKV], F32, ctx)
        QT = sb(f"QT_{tag}", [P, NT * P], F32, ctx)
        KT = sb(f"KT_{tag}", [P, QB + NT * P], F32, ctx)
        KE = sb(f"KE_{tag}", [P, H, QB + NT * P], F32, ctx)
        V2 = sb(f"V2_{tag}", [P, NB + 1, VW], F32, ctx)
        AOUT = sb(f"AOUT_{tag}", [P, NT, C], F32, ctx)

        with ExitStack() as c:
            T = ln_tiles(lambda n, shape: sb(f"{n}_{tag}", shape, F32, c), NT, sb(f"xn_{tag}", [P, NT, C], F32, c))
            XT = sb(f"XT_{tag}", [P, NT * P], F32, c)
            normed, turned, copied, projected = S("normed"), S("turned"), S("turned_copied"), S("projected")
            NH5 = H + 1
            if rope:
                GAM, COS, SIN = rope
                rms = sb(f"rms_{tag}", [P, 4, NT * NH5], F32, c)
                sq5 = sb(f"sq5_{tag}", [P, NT, NH5 * HD], F32, c)
                rn = sb(f"rn_{tag}", [P, NT, NH5 * HD], F32, c)
                r1 = sb(f"r1_{tag}", [P, NT, NH5, HD // 2], F32, c)
                r2 = sb(f"r2_{tag}", [P, NT, NH5, HD // 2], F32, c)

            with nc.Block() as block:
                @block.vector
                def _(v):
                    layernorm_vector(v, S, X, T)
                    for n in range(NT):
                        v.wait_ge(projected.sem, projected.at(n + 1))
                        v.tensor_copy(QKV[:, n, :], ps[:, 2 + n % 6, 0:NQKV]).then_inc(S("qkv_stored").sem, 1)
                    if rope:
                        chain = S("dve_chain")
                        v.wait_ge(S("qkv_stored").sem, S("qkv_stored").at(NT))
                        v.wait_ge(S("rms_squared").sem, S("rms_squared").at(1))
                        link(v, chain, v.tensor_reduce(rms[:, 0, :], sq5[:].rearrange("p n (h d) -> p (n h) d", d=HD),
                                                       AX_X, ALU.add))
                        v.tensor_scalar(rms[:, 1, :], rms[:, 0, :], 1.0 / HD, RMS_EPS, ALU.mult, ALU.add).then_inc(
                            S("rms_sum").sem, 1)
                        v.wait_ge(S("rms_root").sem, S("rms_root").at(1))
                        link(v, chain, v.reciprocal(rms[:, 3, :], rms[:, 2, :]))
                        QK5 = QKV[:, :, 0:NH5 * HD]
                        link(v, chain, v.tensor_tensor(
                            rn[:].rearrange("p n (h d) -> p n h d", d=HD), QK5.rearrange("p n (h d) -> p n h d", d=HD),
                            over(rms[:, 3, :].rearrange("p (n h) -> p n h", h=NH5), HD), ALU.mult))
                        link(v, chain, v.tensor_tensor(
                            rn[:], rn[:], over_mid(GAM[:].rearrange("p h d -> p (h d)"), NT), ALU.mult))
                        pairs = rn[:].rearrange("p n (h f two) -> p n h f two", two=2, h=NH5)
                        to = QK5.rearrange("p n (h f two) -> p n h f two", two=2, h=NH5)
                        cos = COS[:].unsqueeze(2).to_broadcast([P, NT, NH5, HD // 2])
                        sin = SIN[:].unsqueeze(2).to_broadcast([P, NT, NH5, HD // 2])
                        for part, first, second, op in ((0, cos, sin, ALU.subtract), (1, sin, cos, ALU.add)):
                            v.tensor_tensor(r1[:], pairs[:, :, :, :, 0], first, ALU.mult)
                            link(v, chain, v.tensor_tensor(r2[:], pairs[:, :, :, :, 1], second, ALU.mult))
                            link(v, chain, v.tensor_tensor(to[:, :, :, :, part], r1[:], r2[:], op))

                @block.scalar
                def _(a):
                    layernorm_scalar(a, S, T, ident)
                    for n in range(2):
                        a.wait_ge(turned.sem, turned.at(n + 1))
                        a.activation(XT[:, n * 512:(n + 1) * 512], ps[:, n, :], ACT.Copy).then_inc(copied.sem, 1)
                    if rope:
                        a.wait_ge(S("qkv_stored").sem, S("qkv_stored").at(NT))
                        a.activation(sq5[:], QKV[:, :, 0:NH5 * HD], ACT.Square).then_inc(S("rms_squared").sem, 1)
                        a.wait_ge(S("rms_sum").sem, S("rms_sum").at(1))
                        a.activation(rms[:, 2, :], rms[:, 1, :], ACT.Sqrt).then_inc(S("rms_root").sem, 1)

                @block.tensor
                def _(pe):
                    for n in range(NT):
                        pe.wait_ge(normed.sem, normed.at(n // 4 + 1))
                        m = turn(pe, ps[:, n // 4, (n % 4) * P:(n % 4 + 1) * P], T["xn"][:, n, :], ident[:])
                        if n % 4 == 3:
                            m.then_inc(turned.sem, 1)
                    for n in range(NT):
                        pe.wait_ge(copied.sem, copied.at(n // 4 + 1))
                        if n >= 6:
                            pe.wait_ge(S("qkv_stored").sem, S("qkv_stored").at(n - 5))
                        pe.matmul(ps[:, 2 + n % 6, 0:NQKV], XT[:, n * P:(n + 1) * P], W[:], start=True,
                                  stop=True).then_inc(projected.sem, 1)
            S.close(var_ready=1, std_ready=1, normed=2, turned=2, turned_copied=2,
                    projected=NT, qkv_stored=NT)
            if rope:
                S.close(rms_squared=1, rms_sum=1, rms_root=1)

        with ExitStack() as c:
            K4 = sb(f"K4_{tag}", [P, NT, C], F32, c) if shared_kv else None
            ksrc = K4[:] if shared_kv else QKV[:, :, C:2 * C]
            vsrc = QKV[:, :, (H + 1) * HD:] if shared_kv else QKV[:, :, 2 * C:]
            k4_made, turned, kt_made, cleared = S("k4_made"), S("turned"), S("kt_made"), S("v2_cleared")
            with nc.Block() as block:
                @block.tensor
                def _(pe):
                    for n in range(NT):
                        m = turn(pe, ps[:, n // 4, (n % 4) * P:(n % 4 + 1) * P], QKV[:, n, 0:C], ident[:])
                        if n % 4 == 3:
                            m.then_inc(turned.sem, 1)
                    if shared_kv:
                        pe.wait_ge(k4_made.sem, k4_made.at(1))
                    for n in range(NT):
                        m = turn(pe, ps[:, 2 + n // 4, (n % 4) * P:(n % 4 + 1) * P], ksrc[:, n, :], ident[:])
                        if n % 4 == 3:
                            m.then_inc(turned.sem, 1)

                @block.vector
                def _(v):
                    v.memset(KT[:, 0:QB], 0.0)
                    if shared_kv:
                        v.tensor_copy(K4[:].rearrange("p n (h d) -> p n h d", h=H),
                                      QKV[:, :, H * HD:(H + 1) * HD].unsqueeze(2).to_broadcast([P, NT, H, HD])).then_inc(
                            k4_made.sem, 1)
                    for n in range(2):
                        v.wait_ge(turned.sem, turned.at(n + 3))
                        v.tensor_copy(KT[:, QB + n * 512:QB + (n + 1) * 512], ps[:, 2 + n, :]).then_inc(kt_made.sem, 1)
                    v.wait_ge(kt_made.sem, kt_made.at(2))
                    for h in range(H):
                        v.tensor_scalar(KE[:, h, :], KT[:], heads[:, h:h + 1], None, ALU.mult)

                @block.gpsimd
                def _(g):
                    g.memset(V2[:], 0.0).then_inc(cleared.sem, 1)

                @block.scalar
                def _(a):
                    for n in range(2):
                        a.wait_ge(turned.sem, turned.at(n + 1))
                        a.activation(QT[:, n * 512:(n + 1) * 512], ps[:, n, :], ACT.Copy)
                    a.wait_ge(cleared.sem, cleared.at(1))
                    for j in range(J):
                        src = vsrc[QB * j:QB * (j + 1)]
                        for row, blk in ((QB, j), (0, j + 1)):
                            for hh in range(HC):
                                to = V2[KB * hh + row:KB * hh + row + QB, blk:blk + (NT - 1) * J + 1:J, :]
                                if shared_kv:
                                    a.activation(to, src, ACT.Copy)
                                else:
                                    a.activation(to.rearrange("p n (c hd) -> p n c hd", c=NCH)[:, :, :, hh * HD:(hh + 1) * HD],
                                                 src.rearrange("p n (c hd) -> p n c hd", c=NCH)[:, :, :, hh * HD:(hh + 1) * HD],
                                                 ACT.Copy)
            S.close(turned=4, kt_made=2, v2_cleared=1)
            if shared_kv:
                S.close(k4_made=1)

        with ExitStack() as c:
            SH_ = sb(f"shift_{tag}", [P, 2, H * KB], F32, c)
            PR = sb(f"prob_{tag}", [P, 2, H * KB], F32, c)
            PT = sb(f"probT_{tag}", [P, 2, NCH, P], F32, c)
            MX = sb(f"max_{tag}", [P, 2, H], F32, c)
            DN = sb(f"den_{tag}", [P, 2, H], F32, c)
            RD = sb(f"rden_{tag}", [P, 2, H], F32, c)
            names = ("scored", "w_max", "w_shifted", "w_exp", "w_sum", "w_rden", "p_turned", "p_copied", "attended",
                     "o_stored")
            scored, w_max, shifted, w_exp, w_sum, w_rden, p_turned, p_copied, attended, o_stored = map(S, names)

            def scores(n):
                return ps[:, 2 * (n % 2):2 * (n % 2) + NS, :].rearrange("p s (h k) -> p (s h) k", k=KB)

            def outs(n):
                return ps[:, 6 + n % 2, 0:NCH * J * CD].rearrange("p (c j d) -> p c j d", c=NCH, j=J)

            with nc.Block() as block:
                @block.tensor
                def _(pe):
                    def score(n):
                        if n >= 2:
                            pe.wait_ge(shifted.sem, shifted.at(n - 1))
                        for s in range(NS):
                            bank = ps[:, 2 * (n % 2) + s, :].rearrange("p (h k) -> p h k", k=KB)
                            pe.matmul(bank, identb[:], over_mid(mask[:, 1 if n == 0 else 0, :], SH), start=True,
                                      stop=False, skip_group_check=True)
                            for j in range(J):
                                at = n * P + QB * j
                                m = pe.matmul(bank[QB * j:QB * (j + 1)], QT[:, at:at + QB],
                                              KE[:, s * SH:(s + 1) * SH, at:at + KB], start=False, stop=True,
                                              skip_group_check=True)
                        m.then_inc(scored.sem, 1)

                    score(0)
                    score(1)
                    for n in range(NT):
                        pe.wait_ge(w_exp.sem, w_exp.at(n + 1))
                        if n >= 1:
                            pe.wait_ge(p_copied.sem, p_copied.at(n))
                        for ch in range(NCH):
                            m = turn(pe, ps[:, 4 + ch // 4, (ch % 4) * P:(ch % 4 + 1) * P],
                                     PR[:, n % 2, ch * P:(ch + 1) * P], ident[:])
                        m.then_inc(p_turned.sem, 1)
                        if n + 2 < NT:
                            score(n + 2)
                        pe.wait_ge(p_copied.sem, p_copied.at(n + 1))
                        if n >= 2:
                            pe.wait_ge(o_stored.sem, o_stored.at((n - 1) * J))
                        for ch in range(NCH):
                            v2 = V2[:, n * J:(n + 1) * J, :] if shared_kv else V2[:, n * J:(n + 1) * J, ch * CD:(ch + 1) * CD]
                            m = pe.matmul(outs(n)[:, ch], PT[:, n % 2, ch, :], v2, start=True, stop=True)
                        m.then_inc(attended.sem, 1)

                @block.vector
                def _(v):
                    def softmax_front(n):
                        v.wait_ge(scored.sem, scored.at(n + 1))
                        v.tensor_reduce(MX[:, n % 2, :], scores(n), AX_X, ALU.max).then_inc(w_max.sem, 1)
                        v.wait_ge(w_max.sem, w_max.at(n + 1))
                        if n >= 2:
                            v.wait_ge(w_exp.sem, w_exp.at(n - 1))
                        v.tensor_tensor(SH_[:, n % 2, :].rearrange("p (h k) -> p h k", k=KB), scores(n),
                                        over(MX[:, n % 2, :], KB), ALU.subtract).then_inc(shifted.sem, 1)

                    softmax_front(0)
                    softmax_front(1)
                    for n in range(NT):
                        v.wait_ge(w_exp.sem, w_exp.at(n + 1))
                        v.tensor_reduce(DN[:, n % 2, :], PR[:, n % 2, :].rearrange("p (h k) -> p h k", k=KB), AX_X,
                                        ALU.add).then_inc(w_sum.sem, 1)
                        v.wait_ge(w_sum.sem, w_sum.at(n + 1))
                        v.reciprocal(RD[:, n % 2, :], DN[:, n % 2, :]).then_inc(w_rden.sem, 1)
                        if n + 2 < NT:
                            softmax_front(n + 2)
                        v.wait_ge(w_rden.sem, w_rden.at(n + 1))
                        v.wait_ge(attended.sem, attended.at(n + 1))
                        for j in range(J):
                            rows = slice(QB * j, QB * (j + 1))
                            src = outs(n)[rows, :, j, :]
                            if HC > 1:
                                src = src.rearrange("p c (h d) -> p c h d", h=HC)
                                to = AOUT[rows, n, :].rearrange("p (c h d) -> p c h d", c=NCH, h=HC)
                                rd = over(RD[rows, n % 2, :].rearrange("p (c h) -> p c h", c=NCH), HD)
                            else:
                                to = AOUT[rows, n, :].rearrange("p (c d) -> p c d", c=NCH)
                                rd = over(RD[rows, n % 2, :], HD)
                            v.tensor_tensor(to, src, rd, ALU.mult).then_inc(o_stored.sem, 1)

                @block.scalar
                def _(a):
                    def exps(n):
                        a.wait_ge(shifted.sem, shifted.at(n + 1))
                        if n >= 2:
                            a.wait_ge(p_turned.sem, p_turned.at(n - 1))
                            a.wait_ge(w_sum.sem, w_sum.at(n - 1))
                        a.activation(PR[:, n % 2, :], SH_[:, n % 2, :], ACT.Exp, scale=scale).then_inc(w_exp.sem, 1)

                    exps(0)
                    exps(1)
                    for n in range(NT):
                        a.wait_ge(p_turned.sem, p_turned.at(n + 1))
                        if n >= 2:
                            a.wait_ge(attended.sem, attended.at(n - 1))
                        a.activation(PT[:, n % 2].rearrange("p c q -> p (c q)"),
                                     ps[:, 4:6, :].rearrange("p s c -> p (s c)")[:, 0:NCH * P], ACT.Copy).then_inc(
                            p_copied.sem, 1)
                        if n + 2 < NT:
                            exps(n + 2)
            S.close(**{n: NT for n in names if n != "o_stored"}, o_stored=NT * J)

        with ExitStack() as c:
            AT = sb(f"AT_{tag}", [P, NT * P], F32, c)
            turned, copied, projected = S("turned"), S("turned_copied"), S("projected")
            with nc.Block() as block:
                @block.tensor
                def _(pe):
                    for n in range(NT):
                        m = turn(pe, ps[:, n // 4, (n % 4) * P:(n % 4 + 1) * P], AOUT[:, n, :], ident[:])
                        if n % 4 == 3:
                            m.then_inc(turned.sem, 1)
                    for n in range(NT):
                        pe.wait_ge(copied.sem, copied.at(n // 4 + 1))
                        m = pe.matmul(ps[:, 2 + n // 4, (n % 4) * P:(n % 4 + 1) * P], AT[:, n * P:(n + 1) * P], WO[:],
                                      start=True, stop=True)
                        if n % 4 == 3:
                            m.then_inc(projected.sem, 1)

                @block.scalar
                def _(a):
                    for n in range(2):
                        a.wait_ge(turned.sem, turned.at(n + 1))
                        a.activation(AT[:, n * 512:(n + 1) * 512], ps[:, n, :], ACT.Copy).then_inc(copied.sem, 1)

                @block.vector
                def _(v):
                    for n in range(2):
                        v.wait_ge(projected.sem, projected.at(n + 1))
                        xs = X[:, 4 * n:4 * n + 4, :]
                        v.tensor_tensor(xs, ps[:, 2 + n, :].rearrange("p (n c) -> p n c", n=4), xs, ALU.add)
            S.close(turned=2, turned_copied=2, projected=2)


def ffn(nc, S, ps, X, ident, later, WQK, WVG, WOF, H, DH, E, scale, tag):
    NT = X.shape[1]
    T = NT * P
    ED = E * DH
    HE = H * E
    NEC = ED // P
    G = NT * H
    KT = NT
    NPB = 4

    with ExitStack() as c:
        def sb(name, shape, dt=F32):
            return c.enter_context(nc.sbuf_tensor(f"{name}_{tag}", shape, dt))

        XH = sb("XH", [P, T], F32R)
        XL = sb("XL", [P, T], F32R)
        PROJV = sb("PROJV", [P, NT, E, DH])
        GT = sb("GT", [P, 2, G, E])
        CNT = sb("CNT", [P, 2, G, E], BF16)
        CNTP = sb("CNTP", [P, 2, G, E], BF16)
        GE = sb("GE", [P, E * (E - 1) // 2 * G], BF16)
        SG = sb("SG", [P, NT, HE])
        MIX = sb("MIX", [P, NT, H, E])
        A = sb("A", [P, NT, E, DH])
        WS = [sb(f"WS{i}", [P, 2, 2 * DH], F32R) for i in range(2)]
        QH = [sb(f"QH{i}", [P, T], F32R) for i in range(2)]
        QL = [sb(f"QL{i}", [P, T], F32R) for i in range(2)]
        KHL = [sb(f"KHL{i}", [P, T], F32R) for i in range(2)]
        KH1 = [sb(f"KH1{i}", [P, T], F32R) for i in range(2)]
        NH = [sb(f"NH{i}", [P, NT, 2]) for i in range(2)]
        NM = [sb(f"NM{i}", [P, NT]) for i in range(2)]
        ROW = [sb(f"ROW{i}", [NT, P], F32R) for i in range(2)]
        PB = sb("PB", [P, NPB, T])
        V1 = [sb(f"V1{i}", [P, KT, DH + 1]) for i in range(2)]
        VT = [sb(f"VT{i}", [P, KT // 2, DH]) for i in range(2)]
        OS = [sb(f"OS{i}", [P, NT, DH + 1]) for i in range(2)]
        RDN = sb("RDN", [P, NT])
        MW = sb("MW", [P, NT, E])
        OP = [sb(f"OP{i}", [P, E, DH]) for i in range(2)]
        L = ln_tiles(sb, NT, PB[:, 0, :].rearrange("p (n c) -> p n c", n=NT))
        AT = PB

        turned, hi, lo = S("turned"), S("split_hi"), S("split_lo")
        normed, valued, gated, v_stored, g_stored = map(S, ("normed", "valued", "gated", "v_stored", "g_stored"))
        cnt_set, compared, counted, sigmoid, mixed = S("cnt_set"), S("gates_compared"), S("gates_counted"), S("sigmoid"), S("mixed")
        staged, consts = [S("w_staged0"), S("w_staged1")], S("head_consts")
        m_filled, m_freed = S("m_filled"), S("m_freed")
        qk_hi, kh1 = S("qk_hi"), S("kh1_ready")
        max_ready = S("max_ready")
        row_made, row_set = S("row_made"), S("row_set")
        s_filled, exped, p_freed = S("s_filled"), S("exped"), S("p_freed")
        o_evac, v_step = S("o_evac"), S("v_step")
        o_rden, o_weight, o_prod, o_added = S("o_rden"), S("o_weight"), S("o_prod"), S("o_added")
        a_turned, a_copied, projected = S("a_turned"), S("a_copied"), S("projected")
        R = 2 * NT + 2
        HALVES = {0: 2, 1: 3, 2: 4, 3: 3, 4: 4}
        VS = 2 * E - 1
        M = ps[:, 0:2, :]
        M1 = M.rearrange("p s c -> p (s c)")
        Sb = [ps[:, 2:4, :], ps[:, 4:6, :]]

        def O(t):
            return ps[:, 6 + t // 4, (t % 4) * (DH + 1):(t % 4 + 1) * (DH + 1)]

        NEAR = 2

        def compared_tiles(d):
            first = sum(E - i for i in range(1, d)) * G
            return GE[:, first:first + (E - d) * G].rearrange("p (g e) -> p g e", e=E - d)

        def compare(v, kind, d):
            g = GT[:, kind]
            v.tensor_tensor(compared_tiles(d), g[:, :, 0:E - d], g[:, :, d:E], ALU.is_ge).then_inc(compared.sem, 1)

        def count(eng, chain, cnt, d):
            ge = compared_tiles(d)
            link(eng, chain, eng.tensor_tensor(cnt[:, :, d:E], cnt[:, :, d:E], ge, ALU.add))
            link(eng, chain, eng.tensor_tensor(cnt[:, :, 0:E - d], cnt[:, :, 0:E - d], ge, ALU.subtract))

        def compare_and_count(v, chain, kind):
            for d in range(E - 1, NEAR, -1):
                compare(v, kind, d)
            for d in range(NEAR, 0, -1):
                compare(v, kind, d)
            v.wait_ge(compared.sem, compared.at((kind + 1) * (E - 1)))
            for d in range(1, NEAR + 1):
                count(v, chain, CNT[:, kind], d)

        def counted_by_pool(g, chain, kind):
            for i, d in enumerate(range(E - 1, NEAR, -1)):
                g.wait_ge(compared.sem, compared.at(kind * (E - 1) + i + 1))
                count(g, chain, CNTP[:, kind], d)
            g.sem_inc(counted.sem, 1)

        def counts_joined(v, chain, kind):
            v.wait_ge(counted.sem, counted.at(kind + 1))
            link(v, chain, v.tensor_tensor(CNT[:, kind], CNT[:, kind], CNTP[:, kind], ALU.add))

        with nc.Block() as block:
            @block.sync
            def _(sp):
                def stage(h, p):
                    sp.dma_start(WS[p][:].rearrange("c o d -> c (o d)").bitcast(F32),
                                 WQK[:, bass.ds(h, 1)].rearrange("c o k d -> c (o k d)").bitcast(F32)).then_inc(staged[p].sem, 16)

                def row(h, p):
                    sp.wait_ge(row_made.sem, row_made.at(h + 1))
                    sp.dma_start(QL[p][DH:DH + 1, :].bitcast(F32).rearrange("o (t q) -> o t q", t=NT),
                                 ROW[p][:].bitcast(F32)).then_inc(row_set.sem, 16)

                stage(0, 0)
                stage(1, 1)
                sp.wait_ge(consts.sem, consts.at(1))
                row(0, 0)

                def body(h, p):
                    sp.wait_ge(m_filled.sem, m_filled.at(R * h + 1))
                    stage(h + 2, p)
                    row(h + 1, 1 - p)

                with sp.Fori(0, H // 2 - 1) as i:
                    body(2 * i, 0)
                    body(2 * i + 1, 1)
                row(H - 1, 1)

            @block.gpsimd
            def _(g):
                pool_chain = S("pool_chain")
                for i in range(2):
                    link(g, pool_chain, g.memset(QL[i][DH:, :].bitcast(F32), 0.0))
                g.sem_inc(consts.sem, 1)
                for i in range(2):
                    link(g, pool_chain, g.memset(KH1[i][DH:, :].bitcast(F32), 0.0))
                    link(g, pool_chain, g.memset(KH1[i][DH:DH + 1, :].bitcast(F32), 1.0))
                g.sem_inc(consts.sem, 1)
                for i in range(2):
                    link(g, pool_chain, g.memset(V1[i][:, :, DH:DH + 1], 1.0))
                g.memset(A[:], 0.0).then_inc(consts.sem, 1)
                link(g, pool_chain, g.memset(CNTP[:], 0.0))
                counted_by_pool(g, pool_chain, 0)

                def mix(h, p):
                    for half in range(2):
                        tiles = slice(half * KT // 2, (half + 1) * KT // 2)
                        weight = MIX[:, tiles, bass.ds(h, 1), :].rearrange("p n o e -> p n (o e)")
                        to = V1[p][:, tiles, 0:DH]
                        done = VS * (2 * h + half)
                        g.tensor_tensor(to, PROJV[:, tiles, 0, :], over(weight[:, :, 0], DH), ALU.mult).then_inc(
                            v_step.sem, 1)
                        g.wait_ge(v_step.sem, v_step.at(done + 1))
                        for e in range(1, E):
                            g.tensor_tensor(VT[e % 2][:], PROJV[:, tiles, e, :], over(weight[:, :, e], DH),
                                            ALU.mult).then_inc(v_step.sem, 1)
                            g.wait_ge(v_step.sem, v_step.at(done + 2 * e))
                            g.tensor_tensor(to, to, VT[e % 2][:], ALU.add).then_inc(v_step.sem, 1)

                g.wait_ge(v_stored.sem, v_stored.at(NT))
                g.wait_ge(mixed.sem, mixed.at(1))
                mix(0, 0)
                counted_by_pool(g, pool_chain, 1)
                mix(1, 1)

                def body(h, p):
                    g.wait_ge(p_freed.sem, p_freed.at(NPB + KT * (h + 1)))
                    mix(h + 2, p)

                with g.Fori(0, H // 2 - 1) as i:
                    body(2 * i, 0)
                    body(2 * i + 1, 1)

            @block.tensor
            def _(pe):
                for n in range(NT):
                    pe.wait_ge(normed.sem, normed.at(n // 4 + 1))
                    m = turn(pe, ps[:, n // 4, (n % 4) * P:(n % 4 + 1) * P], L["xn"][:, n, :], ident[:])
                    if n % 4 == 3:
                        m.then_inc(turned.sem, 1)
                parts = ((XH, 0), (XH, 1), (XL, 0))
                for n in range(NT):
                    pe.wait_ge(lo.sem, lo.at(n // 4 + 1))
                    t = slice(n * P, (n + 1) * P)
                    for k, (xp, w) in enumerate(parts):
                        m = pe.matmul(ps[:, 4 + n // 2, 256 * (n % 2):256 * (n % 2) + 256], xp[:, t],
                                      WVG[:, w, ED:], start=k == 0, stop=k == 2)
                    m.then_inc(gated.sem, 1)

                def values(n):
                    if n >= 2:
                        pe.wait_ge(v_stored.sem, v_stored.at(n - 1))
                    t = slice(n * P, (n + 1) * P)
                    for k, (xp, w) in enumerate(parts):
                        m = pe.matmul(ps[:, 2 + n % 2, :], xp[:, t], WVG[:, w, 0:ED], start=k == 0, stop=k == 2)
                    m.then_inc(valued.sem, 1)

                def project(h, p):
                    if not (isinstance(h, int) and h == 0):
                        pe.wait_ge(m_freed.sem, m_freed.at(R * h))
                    pe.wait_ge(staged[p].sem, staged[p].at(8 * (h - p) + 16))
                    for k, (w, xp) in enumerate(((0, XH), (0, XL), (1, XH))):
                        for half in range(2):
                            m = pe.matmul(M[:, half, :], WS[p][:, w, :], xp[:, half * 512:(half + 1) * 512],
                                          start=k == 0, stop=k == 2)
                    m.then_inc(m_filled.sem, 1)

                def max_scores(h, p, i):
                    pe.wait_ge(m_freed.sem, m_freed.at(R * h + max(i, 1)))
                    pe.matmul(M[:, i % 2, :], QH[p][:, (i // 2) * P:(i // 2 + 1) * P],
                              KHL[p][:, (i % 2) * 512:(i % 2 + 1) * 512], start=True, stop=True).then_inc(
                        m_filled.sem, 1)

                def max_turn(h, p):
                    pe.wait_ge(max_ready.sem, max_ready.at(h + 1))
                    turn(pe, M[0:NT, 0, 0:P], NM[p][:], ident[:]).then_inc(m_filled.sem, 1)

                def scores(h, p, k):
                    n = KT * h + k
                    pe.wait_ge(exped.sem, exped.at(n + 1))
                    if isinstance(h, int) and h == 0 and k == 0:
                        pe.wait_ge(consts.sem, consts.at(2))
                        pe.wait_ge(v_stored.sem, v_stored.at(NT))
                        pe.wait_ge(g_stored.sem, g_stored.at(NT // 2))
                    if k == 0:
                        pe.wait_ge(row_set.sem, row_set.at(16 * (h + 1)))
                        pe.wait_ge(kh1.sem, kh1.at(h + 1))
                    keys = slice(k * P, (k + 1) * P)
                    for half in range(2):
                        pe.matmul(Sb[k % 2][:, half, :], KHL[p][:, keys], QH[p][:, half * 512:(half + 1) * 512],
                                  start=True, stop=False)
                    for half in range(2):
                        m = pe.matmul(Sb[k % 2][:, half, :], KH1[p][:, keys],
                                      QL[p][:, half * 512:(half + 1) * 512], start=False, stop=True)
                    m.then_inc(s_filled.sem, 1)

                def attend(p, k, tiles):
                    for t in tiles:
                        m = pe.matmul(O(t), PB[:, k % NPB, t * P:(t + 1) * P], V1[p][:, k, :],
                                      start=(k == 0 and t % 4 == 0), stop=(k == KT - 1), skip_group_check=True)
                    return m

                def body(h, p, more=True, project_next=True):
                    i = 0
                    for k in range(KT):
                        if k + 1 < KT:
                            scores(h, p, k + 1)
                        elif more:
                            scores(h + 1, 1 - p, 0)
                        if project_next and k == KT - 2:
                            project(h + 2, p)
                        pe.wait_ge(exped.sem, exped.at(2 + KT * h + k + 1))
                        if k % (KT // 2) == 0:
                            pe.wait_ge(v_step.sem, v_step.at(VS * (2 * h + 1 + k // (KT // 2))))
                        if k == 0:
                            pe.wait_ge(o_evac.sem, o_evac.at(h + 1))
                        for part in range(4):
                            m = attend(p, k, range(2 * part, 2 * part + 2))
                            if part == 3:
                                m.then_inc(p_freed.sem, 1)
                            if more and part >= 4 - HALVES.get(k, 0):
                                max_scores(h + 1, 1 - p, i)
                                i += 1
                            if more and k == 5 and part == 2:
                                max_turn(h + 1, 1 - p)

                pe.sem_inc(p_freed.sem, NPB)
                project(0, 0)
                for n in range(NT):
                    values(n)
                for i in range(2 * NT):
                    max_scores(0, 0, i)
                max_turn(0, 0)
                project(1, 1)
                scores(0, 0, 0)
                with pe.Fori(0, H // 2 - 1) as i:
                    body(2 * i, 0)
                    body(2 * i + 1, 1)
                body(H - 2, 0, project_next=False)
                body(H - 1, 1, more=False, project_next=False)

                pe.wait_ge(exped.sem, exped.at(2 + KT * H))
                pe.wait_ge(m_freed.sem, m_freed.at(R * H))

                def a_turn(n):
                    pe.wait_ge(o_added.sem, o_added.at(NT * (H + 1) + n + 1))
                    if n >= 4:
                        pe.wait_ge(a_copied.sem, a_copied.at(n - 3))
                    for ec in range(NEC):
                        m = turn(pe, ps[:, 2 + n % 4, ec * P:(ec + 1) * P],
                                 A[:, n].rearrange("p e d -> p (e d)")[:, ec * P:(ec + 1) * P], ident[:])
                    m.then_inc(a_turned.sem, 1)

                a_turn(0)
                for n in range(NT):
                    if n + 1 < NT:
                        a_turn(n + 1)
                    pe.wait_ge(a_copied.sem, a_copied.at(n + 1))
                    for ec in range(NEC):
                        m = pe.matmul(ps[:, n // 4, (n % 4) * P:(n % 4 + 1) * P], AT[:, ec, n * P:(n + 1) * P],
                                      WOF[:, ec, :], start=ec == 0, stop=ec == NEC - 1)
                    m.then_inc(projected.sem, 1)

            @block.scalar
            def _(a):
                layernorm_scalar(a, S, L, ident)
                for n in range(2):
                    a.wait_ge(turned.sem, turned.at(n + 1))
                    a.activation(XH[:, n * 512:(n + 1) * 512], ps[:, n, :], ACT.Copy).then_inc(hi.sem, 1)
                a.activation(L["warm"][:], ident[:, 0:1], ACT.Exp)

                def q_high(h, p):
                    a.wait_ge(m_filled.sem, m_filled.at(R * h + 1))
                    a.activation(QH[p][0:DH, :], M1[0:DH], ACT.Copy, scale=scale)
                    a.activation(QH[p][DH:2 * DH, :], M1[0:DH], ACT.Copy, scale=scale)

                def k_high(p):
                    a.activation(KHL[p][0:DH, :], M1[DH:2 * DH], ACT.Copy).then_inc(qk_hi.sem, 1)

                def k_high_again(h, p):
                    a.wait_ge(qk_hi.sem, qk_hi.at(h + 1))
                    a.activation(KH1[p][0:DH, :], KHL[p][0:DH, :].bitcast(F32), ACT.Copy).then_inc(kh1.sem, 1)

                def row(h, p, reused=True):
                    a.wait_ge(m_filled.sem, m_filled.at(R * (h + 1)))
                    if reused:
                        a.wait_ge(row_set.sem, row_set.at(16 * h))
                    a.activation(ROW[p][:], M[0:NT, 0, 0:P], ACT.Copy).then_inc(row_made.sem, 1)
                    a.wait_ge(row_made.sem, row_made.at(h + 1))
                    a.sem_inc(m_freed.sem, 1)

                def exp(h, k):
                    a.wait_ge(s_filled.sem, s_filled.at(KT * h + k + 1))
                    a.wait_ge(p_freed.sem, p_freed.at(KT * h + k + 1))
                    a.activation(PB[:, k % NPB, :], Sb[k % 2].rearrange("p s c -> p (s c)"), ACT.Exp).then_inc(
                        exped.sem, 1)

                def evacuate(h, p):
                    a.wait_ge(p_freed.sem, p_freed.at(NPB + KT * (h + 1)))
                    a.wait_ge(o_added.sem, o_added.at(NT * (h + 1)))
                    for half in range(2):
                        m = a.activation(OS[p][:, 4 * half:4 * half + 4, :].rearrange("p t d -> p (t d)"),
                                         ps[:, 6 + half, 0:4 * (DH + 1)], ACT.Copy)
                    m.then_inc(o_evac.sem, 1)

                def body(h, p, more=True, project_next=True):
                    exp(h, 1)
                    exp(h, 2)
                    if more:
                        k_high_again(h + 1, 1 - p)
                    for k in range(3, KT):
                        exp(h, k)
                        if more and k == KT - 2:
                            row(h + 1, 1 - p)
                    if project_next:
                        q_high(h + 2, p)
                        k_high(p)
                    if more:
                        exp(h + 1, 0)
                    evacuate(h, p)

                a.sem_inc(exped.sem, 2)
                a.sem_inc(o_evac.sem, 1)
                a.wait_ge(g_stored.sem, g_stored.at(NT // 2))
                gates = GT[:, 0].rearrange("p (n h) e -> p n (h e)", n=NT)
                a.activation(SG[:], gates, ACT.Exp, scale=-1.0).then_inc(sigmoid.sem, 1)
                q_high(0, 0)
                k_high(0)
                for n in range(NT):
                    a.wait_ge(valued.sem, valued.at(n + 1))
                    a.activation(PROJV[:, n].rearrange("p e d -> p (e d)"), ps[:, 2 + n % 2, :], ACT.Copy).then_inc(
                        v_stored.sem, 1)
                a.wait_ge(sigmoid.sem, sigmoid.at(1))
                a.activation(SG[:], SG[:], ACT.Ln, bias=1.0).then_inc(sigmoid.sem, 1)
                a.wait_ge(sigmoid.sem, sigmoid.at(2))
                a.activation(SG[:], SG[:], ACT.Exp, scale=-1.0).then_inc(sigmoid.sem, 1)
                k_high_again(0, 0)
                row(0, 0, reused=False)
                q_high(1, 1)
                k_high(1)
                exp(0, 0)
                with a.Fori(0, H // 2 - 1) as i:
                    body(2 * i, 0)
                    body(2 * i + 1, 1)
                body(H - 2, 0, project_next=False)
                body(H - 1, 1, more=False, project_next=False)

                a.wait_ge(p_freed.sem, p_freed.at(NPB + KT * H))
                for n in range(NT):
                    a.wait_ge(a_turned.sem, a_turned.at(n + 1))
                    a.activation(AT[:, :, n * P:(n + 1) * P], ps[:, 2 + n % 4, :].rearrange("p (e q) -> p e q", e=NEC),
                                 ACT.Copy).then_inc(a_copied.sem, 1)

            @block.vector
            def _(v):
                chain = S("dve_chain")
                layernorm_vector(v, S, X, L)
                v.tensor_copy(CNT[:].rearrange("p k g e -> p (k g) e"), over_mid(later[:], 2 * G)).then_inc(
                    cnt_set.sem, 1)
                for n in range(2):
                    v.wait_ge(hi.sem, hi.at(n + 1))
                    v.tensor_tensor(XL[:, n * 512:(n + 1) * 512], ps[:, n, :],
                                    XH[:, n * 512:(n + 1) * 512].bitcast(F32), ALU.subtract).then_inc(lo.sem, 1)
                for n in range(NT // 2):
                    v.wait_ge(gated.sem, gated.at(2 * n + 2))
                    v.tensor_copy(GT[:, :, 2 * n * H:(2 * n + 2) * H, :].rearrange("p k (n h) e -> p k n (h e)", n=2),
                                  ps[:, 4 + n, :].rearrange("p (n k g) -> p k n g", n=2, k=2)).then_inc(g_stored.sem, 1)
                v.wait_ge(g_stored.sem, g_stored.at(NT // 2))
                v.wait_ge(cnt_set.sem, cnt_set.at(1))
                compare_and_count(v, chain, 0)

                v.sem_inc(o_added.sem, 2 * NT)

                def low(h, p):
                    v.wait_ge(qk_hi.sem, qk_hi.at(h + 1))
                    v.scalar_tensor_tensor(QL[p][0:DH, :], M1[0:DH], scale, QH[p][0:DH, :].bitcast(F32),
                                           ALU.mult, ALU.subtract)
                    v.tensor_tensor(KHL[p][DH:2 * DH, :], M1[DH:2 * DH], KHL[p][0:DH, :].bitcast(F32),
                                    ALU.subtract).then_inc(m_freed.sem, 1)

                def maximum(h, p, i):
                    v.wait_ge(m_filled.sem, m_filled.at(R * h + 2 + i))
                    v.tensor_reduce(NH[p][:, i // 2, i % 2:i % 2 + 1], M[:, i % 2, :], AX_X,
                                    ALU.max).then_inc(m_freed.sem, 1)

                def maxima(h, p):
                    v.wait_ge(m_freed.sem, m_freed.at(R * h + 1 + 2 * NT))
                    v.tensor_reduce(NM[p][:], NH[p][:], AX_X, ALU.max, negate=True).then_inc(max_ready.sem, 1)

                def weights(h, p):
                    v.wait_ge(o_evac.sem, o_evac.at(h + 2))
                    v.reciprocal(RDN[:], OS[p][:, :, DH]).then_inc(o_rden.sem, 1)
                    v.wait_ge(o_rden.sem, o_rden.at(h + 1))
                    before = CNT[:, 1].rearrange("p (n h) e -> p n h e", n=NT)[:, :, bass.ds(h, 1), :].rearrange(
                        "p n o e -> p n (o e)")
                    v.scalar_tensor_tensor(MW[:], before, 2.0, over(RDN[:], E), ALU.is_lt, ALU.mult).then_inc(o_weight.sem, 1)
                    v.wait_ge(o_weight.sem, o_weight.at(h + 1))

                def product(h, p, t):
                    v.wait_ge(o_added.sem, o_added.at(NT * (h + 2) + t - 1))
                    v.tensor_tensor(OP[t % 2][:], over_mid(OS[p][:, t, 0:DH], E), over(MW[:, t, :], DH),
                                    ALU.mult).then_inc(o_prod.sem, 1)

                def added(h, t):
                    v.wait_ge(o_prod.sem, o_prod.at(NT * h + t + 1))
                    v.tensor_tensor(A[:, t], A[:, t], OP[t % 2][:], ALU.add).then_inc(o_added.sem, 1)

                def sum_steps(h, p):
                    yield lambda: product(h, p, 0)
                    for t in range(NT):
                        if t + 1 < NT:
                            yield lambda t=t: product(h, p, t + 1)
                        yield lambda t=t: added(h, t)

                def body(h, p):
                    low(h + 1, 1 - p)
                    maximum(h + 1, 1 - p, 0)
                    maximum(h + 1, 1 - p, 1)
                    weights(h - 1, 1 - p)
                    steps = sum_steps(h - 1, 1 - p)
                    for i in range(2, 2 * NT):
                        if i % 2 == 0:
                            next(steps)()
                        maximum(h + 1, 1 - p, i)
                    maxima(h + 1, 1 - p)
                    for step in steps:
                        step()

                low(0, 0)
                for i in range(2 * NT):
                    maximum(0, 0, i)
                    if i == NT // 2:
                        counts_joined(v, chain, 0)
                        v.wait_ge(sigmoid.sem, sigmoid.at(3))
                        v.scalar_tensor_tensor(MIX[:].rearrange("p n h e -> p n (h e)"),
                                               CNT[:, 0].rearrange("p (n h) e -> p n (h e)", n=NT), 2.0, SG[:],
                                               ALU.is_lt, ALU.mult).then_inc(mixed.sem, 1)
                maxima(0, 0)
                compare_and_count(v, chain, 1)
                low(1, 1)
                for i in range(2 * NT):
                    maximum(1, 1, i)
                maxima(1, 1)
                counts_joined(v, chain, 1)
                v.wait_ge(consts.sem, consts.at(3))
                with v.Fori(0, H // 2 - 1) as i:
                    body(2 * i + 1, 1)
                    body(2 * i + 2, 0)
                for h in range(H - 2, H):
                    weights(h, h % 2)
                    for step in sum_steps(h, h % 2):
                        step()

                for n in range(2):
                    v.wait_ge(projected.sem, projected.at(4 * n + 4))
                    xs = X[:, 4 * n:4 * n + 4, :]
                    v.tensor_tensor(xs, ps[:, n, :].rearrange("p (n c) -> p n c", n=4), xs, ALU.add)
        S.close(var_ready=1, std_ready=1, normed=2, turned=2, split_hi=2, split_lo=2,
                valued=NT, gated=NT, v_stored=NT, g_stored=NT // 2, cnt_set=1, gates_compared=2 * (E - 1), gates_counted=2, sigmoid=3, mixed=1)
        S.close(w_staged0=8 * H, w_staged1=8 * H, head_consts=3, m_filled=R * H, m_freed=R * H, qk_hi=H, kh1_ready=H,
                row_made=H, max_ready=H, row_set=16 * H, s_filled=KT * H, exped=2 + KT * H, p_freed=NPB + KT * H,
                o_evac=H + 1, v_step=2 * VS * H, o_rden=H, o_weight=H, o_prod=NT * H, o_added=NT * (H + 2))
        S.close(a_turned=NT, a_copied=NT, projected=NT)


_INS = ["L0_attn_a_x", "L0_attn_a_Wq", "L0_attn_a_Wk", "L0_attn_a_Wv", "L0_attn_a_Wo", "L0_attn_a_q_gamma",
        "L0_attn_a_k_gamma", "L0_attn_b_wq", "L0_attn_b_wk", "L0_attn_b_wv", "L0_attn_b_wo", "L0_ffn_Wq",
        "L0_ffn_Wk", "L0_ffn_Wv", "L0_ffn_Ws", "L0_ffn_Wd", "L0_ffn_Wo"]


def rope_tables(T, head_dim):
    exponent = np.arange(0, head_dim, 2, dtype=np.float32) / np.float32(head_dim)
    inv_freq = (np.float32(1.0) / np.power(np.float32(1000000.0), exponent)).astype(np.float32)
    angles = np.outer(np.arange(T, dtype=np.float32), inv_freq).astype(np.float32)
    return np.cos(angles.astype(np.float64)).astype(np.float32), np.sin(angles.astype(np.float64)).astype(np.float32)


def kernel(**inputs):
    import concourse.bacc as _bacc
    from concourse.bass_utils import run_bass_kernel_spmd as _run

    nc = _bacc.Bacc("TRN2", target_bir_lowering=False, num_devices=1)
    arrays, args = {}, {}
    for name in _INS:
        a = np.ascontiguousarray(inputs[name])
        arrays[f"in_{name}_dram"] = a
        args[name] = nc.dram_tensor(f"in_{name}_dram", a.shape, mybir.dt.from_np(a.dtype), kind="ExternalInput").ap()
    shape = args["L0_attn_a_x"].shape
    cos, sin = rope_tables(shape[1], 32)
    for name, a in (("rope_cos", cos), ("rope_sin", sin)):
        arrays[f"in_{name}_dram"] = a
        args[name] = nc.dram_tensor(f"in_{name}_dram", a.shape, mybir.dt.from_np(a.dtype), kind="ExternalInput").ap()
    out = nc.dram_tensor("out_0_dram", shape, F32, kind="ExternalOutput").ap()
    build(nc, args, out)
    r = _run(nc, [arrays], core_ids=[0])
    return r.results[0]["out_0_dram"]
```

```python
from contextlib import ExitStack
from itertools import islice

import numpy as np

import concourse.bass as bass
from concourse import mybir

ALU = mybir.AluOpType
ACT = mybir.ActivationFunctionType
AX_X = mybir.AxisListType.X
F32 = mybir.dt.float32
F32R = mybir.dt.float32r
BF16 = mybir.dt.bfloat16

P = 128
C = 128
LN_EPS = 1e-5
RMS_EPS = 1e-6
NEG = -1e30


class Signal:

    def __init__(self, ctx, nc, name):
        self.sem = ctx.enter_context(nc.semaphore(name))
        self.base = 0

    def at(self, k):
        return self.base + k


class Signals:

    def __init__(self, ctx, nc):
        self.ctx, self.nc, self.all = ctx, nc, {}

    def __call__(self, name):
        if name not in self.all:
            self.all[name] = Signal(self.ctx, self.nc, name)
        return self.all[name]

    def close(self, **made):
        for name, n in made.items():
            self.all[name].base += n


def link(eng, sig, ins):
    ins.then_inc(sig.sem, 1)
    sig.base += 1
    eng.wait_ge(sig.sem, sig.base)


def over(ap, n):
    return ap.unsqueeze(len(ap.shape)).to_broadcast(list(ap.shape) + [n])


def over_mid(ap, n):
    return ap.unsqueeze(1).to_broadcast([ap.shape[0], n] + list(ap.shape[1:]))


def turn(pe, out, block, ident):
    return pe.matmul(out, block, ident, start=True, stop=True)


def keep_clock(pe, bank, identb, n):
    for _ in range(n):
        pe.matmul(bank, identb[:], over_mid(identb[:], 4), start=True, stop=True)


def layernorm_vector(v, S, X, T):
    chain = S("dve_chain")
    NT = X.shape[1]
    for n in range(NT):
        m = v.bn_stats(T["stats"][:, n, :], X[:, n, :])
    link(v, chain, m)
    for n in range(NT):
        m = v.bn_aggr(T["mean_var"][:, n, :], T["stats"][:, n, :])
    link(v, chain, m)
    v.tensor_scalar(T["var"][:], T["mean_var"][:, :, 1], LN_EPS, None, ALU.add).then_inc(S("var_ready").sem, 1)
    v.wait_ge(S("std_ready").sem, S("std_ready").at(1))
    link(v, chain, v.reciprocal(T["rstd"][:], T["std"][:]))
    for n in range(NT):
        m = v.tensor_scalar(T["xn"][:, n, :], X[:, n, :], T["mean_var"][:, n, 0:1], T["rstd"][:, n:n + 1],
                            ALU.subtract, ALU.mult)
        if n % (NT // 2) == NT // 2 - 1:
            m.then_inc(S("normed").sem, 1)


def layernorm_scalar(a, S, T, ident):
    a.activation(T["warm"][:], ident[:, 0:1], ACT.Sqrt)
    a.wait_ge(S("var_ready").sem, S("var_ready").at(1))
    a.activation(T["std"][:], T["var"][:], ACT.Sqrt).then_inc(S("std_ready").sem, 1)


def build(nc, IN, out):
    x_in = IN["L0_attn_a_x"]
    B, T, _ = x_in.shape
    NT = T // P
    HF, DH, _ = IN["L0_ffn_Wq"].shape
    E = IN["L0_ffn_Wv"].shape[0]
    ED = E * DH
    NEC = ED // P
    HE = HF * E
    FFN_SCALE = float(DH) ** -0.5

    with ExitStack() as ctx:
        def sb(name, shape, dt=F32, c=ctx):
            return c.enter_context(nc.sbuf_tensor(name, shape, dt))

        S = Signals(ctx, nc)
        ps = ctx.enter_context(nc.psum_tensor("ps", [P, 8, 512], F32))

        X = sb("X", [P, B * NT, C])
        ident = sb("ident", [P, P])
        identb = sb("identb", [P, P], BF16)
        later = sb("later", [P, E], BF16)
        WQK = sb("WQK", [P, HF, 2, 2 * DH], F32R)
        WVG = sb("WVG", [P, 2, ED + 2 * HE], F32R)
        WOF = sb("WOF", [P, NEC, C])
        GAM = sb("GAM", [P, 5, 32])
        COS = sb("COS", [P, NT, 16])
        SIN = sb("SIN", [P, NT, 16])

        A_H, A_HD, A_QB, A_LO = 4, 32, 64, 0
        B_H, B_HD, B_QB, B_LO = 16, 8, 32, 1
        WA = sb("WA", [P, 192])
        WOA = sb("WOA", [P, C])
        WB = sb("WB", [P, 3 * C])
        WOB = sb("WOB", [P, C])
        masks = {"a": sb("mask_a", [P, 2, 2 * A_QB], BF16), "b": sb("mask_b", [P, 2, 2 * B_QB], BF16)}
        heads = {"a": sb("heads_a", [P, A_H]), "b": sb("heads_b", [P, B_H])}

        with ExitStack() as c:
            raw = sb("raw", [P, 30, C], F32, c)
            Q0, K0, V0, S0, D0, O0, AQ, AKV, AO, BQ = 0, 8, 16, 20, 21, 22, 26, 27, 28, 29
            rawb = sb("rawb", [P, 3, C], F32, c)
            loads = []

            def load(dst, src):
                loads.append((dst, src))

            load(raw[:, Q0:Q0 + 8, :], IN["L0_ffn_Wq"].rearrange("h d c -> (h d) c").rearrange("(n p) c -> p n c", p=P))
            load(raw[:, K0:K0 + 8, :], IN["L0_ffn_Wk"].rearrange("h d c -> (h d) c").rearrange("(n p) c -> p n c", p=P))
            n_first = len(loads)
            load(raw[:, V0:V0 + 4, :], IN["L0_ffn_Wv"].rearrange("h d c -> (h d) c").rearrange("(n p) c -> p n c", p=P))
            load(raw[:, S0, :], IN["L0_ffn_Ws"].rearrange("h e c -> (h e) c"))
            load(raw[:, D0, :], IN["L0_ffn_Wd"].rearrange("h e c -> (h e) c"))
            load(raw[:, O0:O0 + 4, :].rearrange("f n (e d) -> f (n e) d", d=DH), IN["L0_ffn_Wo"].rearrange("e f d -> f e d"))
            load(raw[:, AQ, :], IN["L0_attn_a_Wq"])
            load(raw[0:32, AKV, :], IN["L0_attn_a_Wk"])
            load(raw[32:64, AKV, :], IN["L0_attn_a_Wv"])
            load(raw[:, AO, :], IN["L0_attn_a_Wo"])
            load(raw[:, BQ, :], IN["L0_attn_b_wq"])
            load(rawb[:, 0, :], IN["L0_attn_b_wk"])
            load(rawb[:, 1, :], IN["L0_attn_b_wv"])
            load(rawb[:, 2, :], IN["L0_attn_b_wo"])
            for n in range(4):
                load(GAM[:, n, :], IN["L0_attn_a_q_gamma"].rearrange("(a d) -> a d", a=1).to_broadcast([P, 32]))
            load(GAM[:, 4, :], IN["L0_attn_a_k_gamma"].rearrange("(a d) -> a d", a=1).to_broadcast([P, 32]))
            load(COS[:], IN["rope_cos"].rearrange("(n p) f -> p n f", p=P))
            load(SIN[:], IN["rope_sin"].rearrange("(n p) f -> p n f", p=P))
            for b in range(B):
                load(X[:, b * NT:(b + 1) * NT, :], x_in[b].rearrange("(n p) c -> p n c", p=P))
            n_loads = len(loads)
            first_loaded = S("first_loaded")
            loaded, made, turned, split, moved = S("loaded"), S("const_made"), S("turned"), S("split_hi"), S("bank_freed")

            with nc.Block() as block:
                @block.sync
                def _(sp):
                    for i in range(0, n_loads, 2):
                        sp.dma_start(*loads[i]).then_inc((first_loaded if i < n_first else loaded).sem, 16)

                @block.gpsimd
                def _(g):
                    chain = S("pool_chain")
                    link(g, chain, g.memset(ident[:], 0.0))
                    link(g, chain, g.affine_select(out=ident[:], in_=ident[:], compare_op=ALU.not_equal, fill=1.0,
                                                   base=0, pattern=[[-1, P]], channel_multiplier=1))
                    g.tensor_copy(identb[:], ident[:]).then_inc(made.sem, 1)
                    for key, QB, H, HD, LO in (("a", A_QB, A_H, A_HD, A_LO), ("b", B_QB, B_H, B_HD, B_LO)):
                        m, KB = masks[key], 2 * QB
                        link(g, chain, g.memset(m[:], 0.0))
                        for j in range(P // QB):
                            v = m[QB * j:QB * (j + 1), :, :]
                            link(g, chain, g.affine_select(out=v, in_=v, compare_op=ALU.is_ge, fill=NEG, base=-LO,
                                                           pattern=[[0, 2], [1, KB]], channel_multiplier=-1))
                            link(g, chain, g.affine_select(out=v, in_=v, compare_op=ALU.is_ge, fill=NEG, base=QB,
                                                           pattern=[[0, 2], [-1, KB]], channel_multiplier=1))
                        v = m[0:QB, 1, :]
                        link(g, chain, g.affine_select(out=v, in_=v, compare_op=ALU.is_ge, fill=NEG, base=-QB,
                                                       pattern=[[1, KB]], channel_multiplier=0))
                        h = heads[key]
                        link(g, chain, g.memset(h[:], 1.0))
                        link(g, chain, g.affine_select(out=h[:], in_=h[:], compare_op=ALU.is_ge, fill=0.0, base=0,
                                                       pattern=[[-HD, H]], channel_multiplier=1))
                        link(g, chain, g.affine_select(out=h[:], in_=h[:], compare_op=ALU.is_ge, fill=0.0, base=HD - 1,
                                                       pattern=[[HD, H]], channel_multiplier=-1))
                    for e in range(E):
                        link(g, chain, g.memset(later[:, e:e + 1], float(E - 1 - e)))

                banks = [[(Q0 + n) for n in range(4)], [(Q0 + 4 + n) for n in range(4)],
                         [(K0 + n) for n in range(4)], [(K0 + 4 + n) for n in range(4)],
                         [(V0 + n) for n in range(4)], [S0, D0, AQ, AO], [(O0 + n) for n in range(4)],
                         [BQ, "wk", "wv", "wo"]]

                @block.tensor
                def _(pe):
                    pe.wait_ge(first_loaded.sem, first_loaded.at(16 * n_first))
                    pe.wait_ge(made.sem, made.at(1))
                    for b, blocks in enumerate(banks):
                        if b == 4:
                            pe.wait_ge(loaded.sem, loaded.at(16 * (n_loads - n_first)))
                        for n, r in enumerate(blocks):
                            src = rawb[:, ("wk", "wv", "wo").index(r), :] if isinstance(r, str) else raw[:, r, :]
                            m = turn(pe, ps[:, b, n * P:(n + 1) * P], src, ident[:])
                        m.then_inc(turned.sem, 1)
                    pe.wait_ge(moved.sem, moved.at(1))
                    turn(pe, ps[:, 0, 0:64], raw[0:64, AKV, :], ident[0:64, 0:64]).then_inc(turned.sem, 1)

                @block.scalar
                def _(a):
                    for i in range(1, n_loads, 2):
                        a.dma_start(*loads[i]).then_inc((first_loaded if i < n_first else loaded).sem, 16)
                    for b in range(4):
                        a.wait_ge(turned.sem, turned.at(b + 1))
                        dst = WQK[:, 8 * (b % 2):8 * (b % 2) + 8, 0, DH * (b // 2):DH * (b // 2) + DH]
                        a.activation(dst, ps[:, b, :].rearrange("c (h d) -> c h d", d=DH), ACT.Copy).then_inc(split.sem, 1)
                    a.wait_ge(turned.sem, turned.at(5))
                    a.activation(WVG[:, 0, 0:ED], ps[:, 4, :], ACT.Copy).then_inc(split.sem, 1)
                    a.wait_ge(turned.sem, turned.at(6))
                    a.activation(WVG[:, 0, ED:], ps[:, 5, 0:2 * HE], ACT.Copy).then_inc(split.sem, 1)

                @block.vector
                def _(v):
                    for b in range(4):
                        v.wait_ge(split.sem, split.at(b + 1))
                        hi = WQK[:, 8 * (b % 2):8 * (b % 2) + 8, 0, DH * (b // 2):DH * (b // 2) + DH]
                        lo = WQK[:, 8 * (b % 2):8 * (b % 2) + 8, 1, DH * (b // 2):DH * (b // 2) + DH]
                        d = v.tensor_tensor(lo, ps[:, b, :].rearrange("c (h d) -> c h d", d=DH), hi.bitcast(F32), ALU.subtract)
                        if b == 0:
                            d.then_inc(moved.sem, 1)
                    v.wait_ge(split.sem, split.at(5))
                    v.tensor_tensor(WVG[:, 1, 0:ED], ps[:, 4, :], WVG[:, 0, 0:ED].bitcast(F32), ALU.subtract)
                    v.wait_ge(split.sem, split.at(6))
                    v.tensor_tensor(WVG[:, 1, ED:], ps[:, 5, 0:2 * HE], WVG[:, 0, ED:].bitcast(F32), ALU.subtract)
                    v.tensor_copy(WA[:, 0:C], ps[:, 5, 2 * P:3 * P])
                    v.tensor_copy(WOA[:], ps[:, 5, 3 * P:4 * P])
                    v.wait_ge(turned.sem, turned.at(7))
                    v.tensor_copy(WOF[:], ps[:, 6, :].rearrange("p (n f) -> p n f", n=NEC))
                    v.wait_ge(turned.sem, turned.at(8))
                    v.tensor_copy(WB[:], ps[:, 7, 0:3 * P])
                    v.tensor_copy(WOB[:], ps[:, 7, 3 * P:4 * P])
                    v.wait_ge(turned.sem, turned.at(9))
                    v.tensor_copy(WA[:, C:C + 64], ps[:, 0, 0:64])
            S.close(first_loaded=16 * n_first, loaded=16 * (n_loads - n_first), const_made=1, turned=9, split_hi=6, bank_freed=1)

        for b in range(B):
            Xb = X[:, b * NT:(b + 1) * NT, :]
            windowed(nc, S, ps, Xb, ident, identb, WA, WOA, masks["a"], heads["a"], H=A_H, HD=A_HD, QB=A_QB,
                     tag=f"a{b}", rope=(GAM, COS, SIN))
            ffn(nc, S, ps, Xb, ident, identb, later, WQK, WVG, WOF, HF, DH, E, FFN_SCALE, tag=f"f{b}")
            windowed(nc, S, ps, Xb, ident, identb, WB, WOB, masks["b"], heads["b"], H=B_H, HD=B_HD, QB=B_QB,
                     tag=f"b{b}", rope=None)
            ffn(nc, S, ps, Xb, ident, identb, later, WQK, WVG, WOF, HF, DH, E, FFN_SCALE, tag=f"g{b}")
            with nc.Block() as block:
                @block.sync
                def _(sp):
                    sp.dma_start(out[b].rearrange("(n p) c -> p n c", p=P), Xb).then_inc(S("stored").sem, 16)
                    if b == B - 1:
                        sp.wait_ge(S("stored").sem, 16 * B)


def ln_tiles(sb, NT, xn):
    shapes = dict(stats=[P, NT, 6], mean_var=[P, NT, 2], var=[P, NT], std=[P, NT], rstd=[P, NT], warm=[P, 1])
    return {"xn": xn} | {n: sb(n, shape) for n, shape in shapes.items()}


def windowed(nc, S, ps, X, ident, identb, W, WO, mask, heads, H, HD, QB, tag, rope):
    NT = X.shape[1]
    J = P // QB
    KB = 2 * QB
    HC = P // KB
    NCH = H // HC
    CD = HC * HD
    NB = NT * J
    shared_kv = rope is not None
    NQKV = W.shape[1]
    scale = float(HD) ** -0.5
    SH = 512 // KB
    NS = H // SH
    VW = HD if shared_kv else C

    def sb(name, shape, dt=F32, c=None):
        return c.enter_context(nc.sbuf_tensor(name, shape, dt))

    with ExitStack() as ctx:
        QT = sb(f"QT_{tag}", [P, NT * P], F32, ctx)
        KT = sb(f"KT_{tag}", [P, QB + NT * P], F32, ctx)
        KE = sb(f"KE_{tag}", [P, H, QB + NT * P], F32, ctx)
        V2 = sb(f"V2_{tag}", [P, NB + 1, VW], F32, ctx)
        AOUT = sb(f"AOUT_{tag}", [P, NT, C], F32, ctx)

        with ExitStack() as c:
            T = ln_tiles(lambda n, shape: sb(f"{n}_{tag}", shape, F32, c), NT, sb(f"xn_{tag}", [P, NT, C], F32, c))
            XT = sb(f"XT_{tag}", [P, NT * P], F32, c)
            normed, turned, copied, projected = S("normed"), S("turned"), S("turned_copied"), S("projected")
            qk_turned, kt_made, cleared = S("qk_turned"), S("kt_made"), S("v2_cleared")
            qkv_stored, rotated, k4_made = S("qkv_stored"), S("rotated"), S("k4_made")
            rms_squared, rms_sum, rms_root = S("rms_squared"), S("rms_sum"), S("rms_root")
            NH5 = H + 1
            POOL_HEADS = 0 if shared_kv else H // 5
            if rope:
                GAM, COS, SIN = rope
                QKV = sb(f"QKV_{tag}", [P, NT, NQKV], F32, c)
                K4 = sb(f"K4_{tag}", [P, NT, C], F32, c)
                rms = sb(f"rms_{tag}", [P, 4, NT * NH5], F32, c)
                sq5 = sb(f"sq5_{tag}", [P, NT, NH5 * HD], F32, c)
                rn = sb(f"rn_{tag}", [P, NT, NH5 * HD], F32, c)
                r1 = sb(f"r1_{tag}", [P, NT, NH5, HD // 2], F32, c)
                r2 = sb(f"r2_{tag}", [P, NT, NH5, HD // 2], F32, c)
                vsrc = QKV[:, :, (H + 1) * HD:]
            else:
                vsrc = ps[:, 6:8, :].rearrange("p s (n c) -> p (s n) c", c=C)

            SH_ = sb(f"shift_{tag}", [P, 2, H * KB], F32, c)
            PR = sb(f"prob_{tag}", [P, 2, H * KB], F32, c)
            PT = sb(f"probT_{tag}", [P, 2, NCH, P], F32, c)
            MX = sb(f"max_{tag}", [P, 2, H], F32, c)
            DN = sb(f"den_{tag}", [P, 2, H], F32, c)
            RD = sb(f"rden_{tag}", [P, 2, H], F32, c)
            AT = sb(f"AT_{tag}", [P, NT * P], F32, c)
            a_turned, a_copied, a_projected = S("a_turned"), S("a_copied"), S("a_projected")
            ke_made, qt_made, v2_made = S("ke_made"), S("qt_made"), S("v2_made")
            names = ("scored", "w_max", "w_shifted", "w_exp", "w_sum", "w_rden", "p_turned", "p_copied", "attended",
                     "o_stored")
            scored, w_max, shifted, w_exp, w_sum, w_rden, p_turned, p_copied, attended, o_stored = map(S, names)

            def scores(n):
                return ps[:, 2 * (n % 2):2 * (n % 2) + NS, :].rearrange("p s (h k) -> p (s h) k", k=KB)

            def outs(n):
                return ps[:, 6 + n % 2, 0:NCH * J * CD].rearrange("p (c j d) -> p c j d", c=NCH, j=J)

            with nc.Block() as block:
                @block.tensor
                def _(pe):
                    keep_clock(pe, ps[:, 7, :], identb, 9)
                    for n in range(NT):
                        pe.wait_ge(normed.sem, normed.at(n // 4 + 1))
                        m = turn(pe, ps[:, n // 4, (n % 4) * P:(n % 4 + 1) * P], T["xn"][:, n, :], ident[:])
                        if n % 4 == 3:
                            m.then_inc(turned.sem, 1)
                    if rope:
                        for n in range(NT):
                            pe.wait_ge(copied.sem, copied.at(n // 4 + 1))
                            if n >= 6:
                                pe.wait_ge(qkv_stored.sem, qkv_stored.at(n - 5))
                            pe.matmul(ps[:, 2 + n % 6, 0:NQKV], XT[:, n * P:(n + 1) * P], W[:], start=True,
                                      stop=True).then_inc(projected.sem, 1)
                        pe.wait_ge(qkv_stored.sem, qkv_stored.at(NT))
                        pe.wait_ge(rotated.sem, rotated.at(1))
                        pe.wait_ge(k4_made.sem, k4_made.at(1))
                        for n in range(NT):
                            m = turn(pe, ps[:, 2 + n // 4, (n % 4) * P:(n % 4 + 1) * P], K4[:, n, :], ident[:])
                            if n % 4 == 3:
                                m.then_inc(qk_turned.sem, 1)
                        for n in range(NT):
                            m = turn(pe, ps[:, n // 4, (n % 4) * P:(n % 4 + 1) * P], QKV[:, n, 0:C], ident[:])
                            if n % 4 == 3:
                                m.then_inc(qk_turned.sem, 1)
                    else:
                        for which in (1, 0):
                            for half in range(2):
                                pe.wait_ge(copied.sem, copied.at(half + 1))
                                pe.matmul(ps[:, 4 - 2 * which + half, :], W[:, which * C:(which + 1) * C],
                                          XT[:, half * 512:(half + 1) * 512], start=True, stop=True).then_inc(
                                    qk_turned.sem, 1)
                        for n in range(NT):
                            m = pe.matmul(ps[:, 6 + n // 4, (n % 4) * P:(n % 4 + 1) * P], XT[:, n * P:(n + 1) * P],
                                          W[:, 2 * C:], start=True, stop=True)
                        m.then_inc(projected.sem, 1)

                    def score(n):
                        if n >= 2:
                            pe.wait_ge(shifted.sem, shifted.at(n - 1))
                        for s in range(NS):
                            bank = ps[:, 2 * (n % 2) + s, :].rearrange("p (h k) -> p h k", k=KB)
                            pe.matmul(bank, identb[:], over_mid(mask[:, 1 if n == 0 else 0, :], SH), start=True,
                                      stop=False, skip_group_check=True)
                            for j in range(J):
                                at = n * P + QB * j
                                m = pe.matmul(bank[QB * j:QB * (j + 1)], QT[:, at:at + QB],
                                              KE[:, s * SH:(s + 1) * SH, at:at + KB], start=False, stop=True,
                                              skip_group_check=True)
                        m.then_inc(scored.sem, 1)

                    pe.wait_ge(ke_made.sem, ke_made.at(2 if POOL_HEADS else 1))
                    pe.wait_ge(qt_made.sem, qt_made.at(2))
                    score(0)
                    score(1)
                    for n in range(NT):
                        pe.wait_ge(w_exp.sem, w_exp.at(n + 1))
                        if n >= 1:
                            pe.wait_ge(p_copied.sem, p_copied.at(n))
                        for ch in range(NCH):
                            m = turn(pe, ps[:, 4 + ch // 4, (ch % 4) * P:(ch % 4 + 1) * P],
                                     PR[:, n % 2, ch * P:(ch + 1) * P], ident[:])
                        m.then_inc(p_turned.sem, 1)
                        if n + 2 < NT:
                            score(n + 2)
                        pe.wait_ge(p_copied.sem, p_copied.at(n + 1))
                        if n == 0:
                            pe.wait_ge(v2_made.sem, v2_made.at(1))
                        if n >= 2:
                            pe.wait_ge(o_stored.sem, o_stored.at((n - 1) * J))
                        for ch in range(NCH):
                            v2 = V2[:, n * J:(n + 1) * J, :] if shared_kv else V2[:, n * J:(n + 1) * J, ch * CD:(ch + 1) * CD]
                            m = pe.matmul(outs(n)[:, ch], PT[:, n % 2, ch, :], v2, start=True, stop=True)
                        m.then_inc(attended.sem, 1)
                    pe.wait_ge(shifted.sem, shifted.at(NT))
                    for n in range(NT):
                        pe.wait_ge(o_stored.sem, o_stored.at((n + 1) * J))
                        m = turn(pe, ps[:, n // 4, (n % 4) * P:(n % 4 + 1) * P], AOUT[:, n, :], ident[:])
                        if n % 4 == 3:
                            m.then_inc(a_turned.sem, 1)
                    for n in range(NT):
                        pe.wait_ge(a_copied.sem, a_copied.at(n // 4 + 1))
                        m = pe.matmul(ps[:, 2 + n // 4, (n % 4) * P:(n % 4 + 1) * P], AT[:, n * P:(n + 1) * P], WO[:],
                                      start=True, stop=True)
                        if n % 4 == 3:
                            m.then_inc(a_projected.sem, 1)

                @block.vector
                def _(v):
                    chain = S("dve_chain")
                    layernorm_vector(v, S, X, T)
                    if rope:
                        v.wait_ge(rms_squared.sem, rms_squared.at(1))
                        link(v, chain, v.tensor_reduce(rms[:, 0, :], sq5[:].rearrange("p n (h d) -> p (n h) d", d=HD),
                                                       AX_X, ALU.add))
                        v.tensor_scalar(rms[:, 1, :], rms[:, 0, :], 1.0 / HD, RMS_EPS, ALU.mult, ALU.add).then_inc(
                            rms_sum.sem, 1)
                        v.wait_ge(rms_root.sem, rms_root.at(1))
                        link(v, chain, v.reciprocal(rms[:, 3, :], rms[:, 2, :]))
                        QK5 = QKV[:, :, 0:NH5 * HD]
                        link(v, chain, v.tensor_tensor(
                            rn[:].rearrange("p n (h d) -> p n h d", d=HD), QK5.rearrange("p n (h d) -> p n h d", d=HD),
                            over(rms[:, 3, :].rearrange("p (n h) -> p n h", h=NH5), HD), ALU.mult))
                        link(v, chain, v.tensor_tensor(
                            rn[:], rn[:], over_mid(GAM[:].rearrange("p h d -> p (h d)"), NT), ALU.mult))
                        pairs = rn[:].rearrange("p n (h f two) -> p n h f two", two=2, h=NH5)
                        to = QK5.rearrange("p n (h f two) -> p n h f two", two=2, h=NH5)
                        cos = COS[:].unsqueeze(2).to_broadcast([P, NT, NH5, HD // 2])
                        sin = SIN[:].unsqueeze(2).to_broadcast([P, NT, NH5, HD // 2])
                        for part, first, second, op in ((0, cos, sin, ALU.subtract), (1, sin, cos, ALU.add)):
                            v.tensor_tensor(r1[:], pairs[:, :, :, :, 0], first, ALU.mult)
                            link(v, chain, v.tensor_tensor(r2[:], pairs[:, :, :, :, 1], second, ALU.mult))
                            link(v, chain, v.tensor_tensor(to[:, :, :, :, part], r1[:], r2[:], op))
                        v.sem_inc(rotated.sem, 1)
                        v.tensor_copy(K4[:].rearrange("p n (h d) -> p n h d", h=H),
                                      QKV[:, :, H * HD:(H + 1) * HD].unsqueeze(2).to_broadcast([P, NT, H, HD])).then_inc(
                            k4_made.sem, 1)
                    for n in range(2):
                        v.wait_ge(qk_turned.sem, qk_turned.at(n + 1))
                        v.tensor_copy(KT[:, QB + n * 512:QB + (n + 1) * 512], ps[:, 2 + n, :]).then_inc(kt_made.sem, 1)
                    v.wait_ge(kt_made.sem, kt_made.at(3))
                    for h in range(POOL_HEADS, H):
                        m = v.tensor_scalar(KE[:, h, :], KT[:], heads[:, h:h + 1], None, ALU.mult)
                    m.then_inc(ke_made.sem, 1)

                    def softmax_front(n):
                        v.wait_ge(scored.sem, scored.at(n + 1))
                        v.tensor_reduce(MX[:, n % 2, :], scores(n), AX_X, ALU.max).then_inc(w_max.sem, 1)
                        v.wait_ge(w_max.sem, w_max.at(n + 1))
                        if n >= 2:
                            v.wait_ge(w_exp.sem, w_exp.at(n - 1))
                        v.tensor_tensor(SH_[:, n % 2, :].rearrange("p (h k) -> p h k", k=KB), scores(n),
                                        over(MX[:, n % 2, :], KB), ALU.subtract).then_inc(shifted.sem, 1)

                    softmax_front(0)
                    softmax_front(1)
                    for n in range(NT):
                        v.wait_ge(w_exp.sem, w_exp.at(n + 1))
                        v.tensor_reduce(DN[:, n % 2, :], PR[:, n % 2, :].rearrange("p (h k) -> p h k", k=KB), AX_X,
                                        ALU.add).then_inc(w_sum.sem, 1)
                        v.wait_ge(w_sum.sem, w_sum.at(n + 1))
                        v.reciprocal(RD[:, n % 2, :], DN[:, n % 2, :]).then_inc(w_rden.sem, 1)
                        if n + 2 < NT:
                            softmax_front(n + 2)
                        v.wait_ge(w_rden.sem, w_rden.at(n + 1))
                        v.wait_ge(attended.sem, attended.at(n + 1))
                        for j in range(J):
                            rows = slice(QB * j, QB * (j + 1))
                            src = outs(n)[rows, :, j, :]
                            if HC > 1:
                                src = src.rearrange("p c (h d) -> p c h d", h=HC)
                                to = AOUT[rows, n, :].rearrange("p (c h d) -> p c h d", c=NCH, h=HC)
                                rd = over(RD[rows, n % 2, :].rearrange("p (c h) -> p c h", c=NCH), HD)
                            else:
                                to = AOUT[rows, n, :].rearrange("p (c d) -> p c d", c=NCH)
                                rd = over(RD[rows, n % 2, :], HD)
                            v.tensor_tensor(to, src, rd, ALU.mult).then_inc(o_stored.sem, 1)
                    for n in range(2):
                        v.wait_ge(a_projected.sem, a_projected.at(n + 1))
                        xs = X[:, 4 * n:4 * n + 4, :]
                        v.tensor_tensor(xs, ps[:, 2 + n, :].rearrange("p (n c) -> p n c", n=4), xs, ALU.add)

                @block.gpsimd
                def _(g):
                    g.memset(V2[:], 0.0).then_inc(cleared.sem, 1)
                    g.memset(KT[:, 0:QB], 0.0).then_inc(kt_made.sem, 1)
                    if POOL_HEADS:
                        g.wait_ge(kt_made.sem, kt_made.at(3))
                        for h in range(POOL_HEADS):
                            m = g.tensor_tensor(KE[:, h, :], KT[:], heads[:, h:h + 1].to_broadcast([P, QB + NT * P]),
                                                ALU.mult)
                        m.then_inc(ke_made.sem, 1)

                @block.scalar
                def _(a):
                    layernorm_scalar(a, S, T, ident)
                    for n in range(2):
                        a.wait_ge(turned.sem, turned.at(n + 1))
                        a.activation(XT[:, n * 512:(n + 1) * 512], ps[:, n, :], ACT.Copy).then_inc(copied.sem, 1)
                    if rope:
                        for n in range(NT):
                            a.wait_ge(projected.sem, projected.at(n + 1))
                            a.activation(QKV[:, n, :], ps[:, 2 + n % 6, 0:NQKV], ACT.Copy).then_inc(qkv_stored.sem, 1)
                        a.wait_ge(qkv_stored.sem, qkv_stored.at(NT))
                        a.activation(sq5[:], QKV[:, :, 0:NH5 * HD], ACT.Square).then_inc(rms_squared.sem, 1)
                        a.wait_ge(rms_sum.sem, rms_sum.at(1))
                        a.activation(rms[:, 2, :], rms[:, 1, :], ACT.Sqrt).then_inc(rms_root.sem, 1)
                    else:
                        for n in range(2):
                            a.wait_ge(qk_turned.sem, qk_turned.at(n + 3))
                            a.activation(QT[:, n * 512:(n + 1) * 512], ps[:, 4 + n, :], ACT.Copy).then_inc(qt_made.sem, 1)
                        a.wait_ge(projected.sem, projected.at(1))
                    a.wait_ge(cleared.sem, cleared.at(1))
                    for j in range(J):
                        src = vsrc[QB * j:QB * (j + 1)]
                        for row, blk in ((QB, j), (0, j + 1)):
                            for hh in range(HC):
                                to = V2[KB * hh + row:KB * hh + row + QB, blk:blk + (NT - 1) * J + 1:J, :]
                                if shared_kv:
                                    m = a.activation(to, src, ACT.Copy)
                                else:
                                    m = a.activation(to.rearrange("p n (c hd) -> p n c hd", c=NCH)[:, :, :, hh * HD:(hh + 1) * HD],
                                                     src.rearrange("p n (c hd) -> p n c hd", c=NCH)[:, :, :, hh * HD:(hh + 1) * HD],
                                                     ACT.Copy)
                    m.then_inc(v2_made.sem, 1)
                    if rope:
                        for n in range(2):
                            a.wait_ge(qk_turned.sem, qk_turned.at(n + 3))
                            a.activation(QT[:, n * 512:(n + 1) * 512], ps[:, n, :], ACT.Copy).then_inc(qt_made.sem, 1)

                    def exps(n):
                        a.wait_ge(shifted.sem, shifted.at(n + 1))
                        if n >= 2:
                            a.wait_ge(p_turned.sem, p_turned.at(n - 1))
                            a.wait_ge(w_sum.sem, w_sum.at(n - 1))
                        a.activation(PR[:, n % 2, :], SH_[:, n % 2, :], ACT.Exp, scale=scale).then_inc(w_exp.sem, 1)

                    exps(0)
                    exps(1)
                    for n in range(NT):
                        a.wait_ge(p_turned.sem, p_turned.at(n + 1))
                        if n >= 2:
                            a.wait_ge(attended.sem, attended.at(n - 1))
                        a.activation(PT[:, n % 2].rearrange("p c q -> p (c q)"),
                                     ps[:, 4:6, :].rearrange("p s c -> p (s c)")[:, 0:NCH * P], ACT.Copy).then_inc(
                            p_copied.sem, 1)
                        if n + 2 < NT:
                            exps(n + 2)
                    for n in range(2):
                        a.wait_ge(a_turned.sem, a_turned.at(n + 1))
                        a.activation(AT[:, n * 512:(n + 1) * 512], ps[:, n, :], ACT.Copy).then_inc(a_copied.sem, 1)
            S.close(var_ready=1, std_ready=1, normed=2, turned=2, turned_copied=2, qk_turned=4, kt_made=3, v2_cleared=1,
                    projected=NT if rope else 1)
            if rope:
                S.close(qkv_stored=NT, rms_squared=1, rms_sum=1, rms_root=1, rotated=1, k4_made=1)
            S.close(**{n: NT for n in names if n != "o_stored"}, o_stored=NT * J,
                    a_turned=2, a_copied=2, a_projected=2, ke_made=2 if POOL_HEADS else 1, qt_made=2, v2_made=1)


def ffn(nc, S, ps, X, ident, identb, later, WQK, WVG, WOF, H, DH, E, scale, tag):
    NT = X.shape[1]
    T = NT * P
    ED = E * DH
    HE = H * E
    NEC = ED // P
    G = NT * H
    KT = NT
    NPB = 4

    with ExitStack() as c:
        def sb(name, shape, dt=F32):
            return c.enter_context(nc.sbuf_tensor(f"{name}_{tag}", shape, dt))

        XH = sb("XH", [P, T], F32R)
        XL = sb("XL", [P, T], F32R)
        PROJV = sb("PROJV", [P, NT, E, DH])
        GT = sb("GT", [P, 2, G, E])
        CNT = sb("CNT", [P, 2, G, E], BF16)
        CNTP = sb("CNTP", [P, G, E], BF16)
        GE = sb("GE", [P, E * (E - 1) // 2 * G], BF16)
        SG = sb("SG", [P, NT, HE])
        MIX = sb("MIX", [P, NT, H, E])
        A = sb("A", [P, NT, E, DH])
        WS = [sb(f"WS{i}", [P, 2, 2 * DH], F32R) for i in range(2)]
        QH = [sb(f"QH{i}", [P, T], F32R) for i in range(2)]
        QL = [sb(f"QL{i}", [P, T], F32R) for i in range(2)]
        KHL = [sb(f"KHL{i}", [P, T], F32R) for i in range(2)]
        KH1 = [sb(f"KH1{i}", [P, T], F32R) for i in range(2)]
        NH = [sb(f"NH{i}", [P, NT, 2]) for i in range(2)]
        NM = [sb(f"NM{i}", [P, NT]) for i in range(2)]
        ROW = [sb(f"ROW{i}", [NT, P], F32R) for i in range(2)]
        PB = sb("PB", [P, NPB, T])
        V1 = [sb(f"V1{i}", [P, KT, DH + 1]) for i in range(2)]
        VT = [sb(f"VT{i}", [P, KT // 2, DH]) for i in range(2)]
        OS = [sb(f"OS{i}", [P, NT, DH + 1]) for i in range(2)]
        RDN = sb("RDN", [P, NT])
        MW = sb("MW", [P, NT, E])
        OP = [sb(f"OP{i}", [P, E, DH]) for i in range(2)]
        L = ln_tiles(sb, NT, PB[:, 0, :].rearrange("p (n c) -> p n c", n=NT))
        AT = PB

        turned, hi, lo = S("turned"), S("split_hi"), S("split_lo")
        normed, valued, gated, v_stored, g_stored = map(S, ("normed", "valued", "gated", "v_stored", "g_stored"))
        cnt_set, compared, counted, mixed = S("cnt_set"), S("gates_compared"), S("gates_counted"), S("mixed")
        sigmoid_step, log_sigmoid, sigmoid = S("sigmoid_step"), S("log_sigmoid"), S("sigmoid")
        staged, consts = [S("w_staged0"), S("w_staged1")], S("head_consts")
        m_filled, m_freed = S("m_filled"), S("m_freed")
        qk_hi, kh1 = S("qk_hi"), S("kh1_ready")
        max_ready = S("max_ready")
        row_made, row_set = S("row_made"), S("row_set")
        s_filled, exped, p_freed = S("s_filled"), S("exped"), S("p_freed")
        o_evac, v_step = S("o_evac"), S("v_step")
        o_rden, o_weight, o_prod, o_added = S("o_rden"), S("o_weight"), S("o_prod"), S("o_added")
        a_turned, a_copied, projected = S("a_turned"), S("a_copied"), S("projected")
        R = 2 * NT + 2
        HALVES = {0: 2, 1: 3, 2: 4, 3: 3, 4: 4}
        SUMS_BEFORE = (2, 4, 9, 11)
        VS = 2 * E - 1
        M = ps[:, 0:2, :]
        M1 = M.rearrange("p s c -> p (s c)")
        Sb = [ps[:, 2:4, :], ps[:, 4:6, :]]

        def first_scores(t):
            return M if t % 2 == 0 else Sb[1]

        def O(t):
            return ps[:, 6 + t // 4, (t % 4) * (DH + 1):(t % 4 + 1) * (DH + 1)]

        NEAR = 2

        def gates_of_bank(n):
            return (GT[:, :, 2 * n * H:(2 * n + 2) * H, :].rearrange("p k (n h) e -> p k n (h e)", n=2),
                    ps[:, 4 + n, :].rearrange("p (n k g) -> p k n g", n=2, k=2))

        def compared_tiles(d):
            first = sum(E - i for i in range(1, d)) * G
            return GE[:, first:first + (E - d) * G].rearrange("p (g e) -> p g e", e=E - d)

        def compare(v, kind, d):
            g = GT[:, kind]
            v.tensor_tensor(compared_tiles(d), g[:, :, 0:E - d], g[:, :, d:E], ALU.is_ge).then_inc(compared.sem, 1)

        def count(eng, chain, cnt, d):
            ge = compared_tiles(d)
            link(eng, chain, eng.tensor_tensor(cnt[:, :, d:E], cnt[:, :, d:E], ge, ALU.add))
            link(eng, chain, eng.tensor_tensor(cnt[:, :, 0:E - d], cnt[:, :, 0:E - d], ge, ALU.subtract))

        def compare_all(v, kind):
            for d in [*range(E - 1, NEAR, -1), *range(NEAR, 0, -1)]:
                compare(v, kind, d)
            v.wait_ge(compared.sem, compared.at((kind + 1) * (E - 1)))

        with nc.Block() as block:
            @block.sync
            def _(sp):
                def stage(h, p):
                    sp.dma_start(WS[p][:].rearrange("c o d -> c (o d)").bitcast(F32),
                                 WQK[:, bass.ds(h, 1)].rearrange("c o k d -> c (o k d)").bitcast(F32)).then_inc(staged[p].sem, 16)

                def row(h, p):
                    sp.wait_ge(row_made.sem, row_made.at(h + 1))
                    sp.dma_start(QL[p][DH:DH + 1, :].bitcast(F32).rearrange("o (t q) -> o t q", t=NT),
                                 ROW[p][:].bitcast(F32)).then_inc(row_set.sem, 16)

                stage(0, 0)
                stage(1, 1)
                sp.wait_ge(consts.sem, consts.at(1))
                row(0, 0)

                def body(h, p):
                    sp.wait_ge(m_filled.sem, m_filled.at(R * h + 1))
                    stage(h + 2, p)
                    row(h + 1, 1 - p)

                with sp.Fori(0, H // 2 - 1) as i:
                    body(2 * i, 0)
                    body(2 * i + 1, 1)
                row(H - 1, 1)

            @block.gpsimd
            def _(g):
                pool_chain = S("pool_chain")
                for i in range(2):
                    link(g, pool_chain, g.memset(QL[i][DH:, :].bitcast(F32), 0.0))
                g.sem_inc(consts.sem, 1)
                for i in range(2):
                    link(g, pool_chain, g.memset(KH1[i][DH:, :].bitcast(F32), 0.0))
                    link(g, pool_chain, g.memset(KH1[i][DH:DH + 1, :].bitcast(F32), 1.0))
                g.sem_inc(consts.sem, 1)
                for i in range(2):
                    link(g, pool_chain, g.memset(V1[i][:, :, DH:DH + 1], 1.0))
                g.memset(A[:], 0.0).then_inc(consts.sem, 1)
                link(g, pool_chain, g.memset(CNTP[:], 0.0))
                for i, d in enumerate(range(E - 1, NEAR, -1)):
                    g.wait_ge(compared.sem, compared.at(i + 1))
                    count(g, pool_chain, CNTP[:], d)
                g.sem_inc(counted.sem, 1)

                def mix(h, p):
                    for half in range(2):
                        tiles = slice(half * KT // 2, (half + 1) * KT // 2)
                        weight = MIX[:, tiles, bass.ds(h, 1), :].rearrange("p n o e -> p n (o e)")
                        to = V1[p][:, tiles, 0:DH]
                        done = VS * (2 * h + half)
                        g.tensor_tensor(to, PROJV[:, tiles, 0, :], over(weight[:, :, 0], DH), ALU.mult).then_inc(
                            v_step.sem, 1)
                        g.wait_ge(v_step.sem, v_step.at(done + 1))
                        for e in range(1, E):
                            g.tensor_tensor(VT[e % 2][:], PROJV[:, tiles, e, :], over(weight[:, :, e], DH),
                                            ALU.mult).then_inc(v_step.sem, 1)
                            g.wait_ge(v_step.sem, v_step.at(done + 2 * e))
                            g.tensor_tensor(to, to, VT[e % 2][:], ALU.add).then_inc(v_step.sem, 1)

                g.wait_ge(v_stored.sem, v_stored.at(NT))
                g.wait_ge(mixed.sem, mixed.at(1))
                mix(0, 0)
                mix(1, 1)

                def body(h, p):
                    g.wait_ge(p_freed.sem, p_freed.at(NPB + KT * (h + 1)))
                    mix(h + 2, p)

                with g.Fori(0, H // 2 - 1) as i:
                    body(2 * i, 0)
                    body(2 * i + 1, 1)

            @block.tensor
            def _(pe):
                keep_clock(pe, ps[:, 7, :], identb, 9)
                for n in range(NT):
                    pe.wait_ge(normed.sem, normed.at(n // 4 + 1))
                    m = turn(pe, ps[:, n // 4, (n % 4) * P:(n % 4 + 1) * P], L["xn"][:, n, :], ident[:])
                    if n % 4 == 3:
                        m.then_inc(turned.sem, 1)
                parts = ((XH, 0), (XH, 1), (XL, 0))
                for n in range(NT):
                    pe.wait_ge(lo.sem, lo.at(n // 4 + 1))
                    t = slice(n * P, (n + 1) * P)
                    for k, (xp, w) in enumerate(parts):
                        m = pe.matmul(ps[:, 4 + n // 2, 256 * (n % 2):256 * (n % 2) + 256], xp[:, t],
                                      WVG[:, w, ED:], start=k == 0, stop=k == 2)
                    m.then_inc(gated.sem, 1)

                def values(n):
                    if n >= 2:
                        pe.wait_ge(v_stored.sem, v_stored.at(n - 1))
                    t = slice(n * P, (n + 1) * P)
                    for k, (xp, w) in enumerate(parts):
                        m = pe.matmul(ps[:, 2 + n % 2, :], xp[:, t], WVG[:, w, 0:ED], start=k == 0, stop=k == 2)
                    m.then_inc(valued.sem, 1)

                def project(h, p):
                    if not (isinstance(h, int) and h == 0):
                        pe.wait_ge(m_freed.sem, m_freed.at(R * h))
                    pe.wait_ge(staged[p].sem, staged[p].at(8 * (h - p) + 16))
                    for k, (w, xp) in enumerate(((0, XH), (0, XL), (1, XH))):
                        for half in range(2):
                            m = pe.matmul(M[:, half, :], WS[p][:, w, :], xp[:, half * 512:(half + 1) * 512],
                                          start=k == 0, stop=k == 2)
                    m.then_inc(m_filled.sem, 1)

                def max_scores(h, p, i):
                    pe.wait_ge(m_freed.sem, m_freed.at(R * h + max(i, 1)))
                    pe.matmul(M[:, i % 2, :], QH[p][:, (i // 2) * P:(i // 2 + 1) * P],
                              KHL[p][:, (i % 2) * 512:(i % 2 + 1) * 512], start=True, stop=True).then_inc(
                        m_filled.sem, 1)

                def max_turn(h, p):
                    pe.wait_ge(max_ready.sem, max_ready.at(h + 1))
                    turn(pe, M[0:NT, 0, 0:P], NM[p][:], ident[:]).then_inc(m_filled.sem, 1)

                def scores(h, p, k):
                    n = KT * h + k
                    pe.wait_ge(exped.sem, exped.at(n + 1))
                    if isinstance(h, int) and h == 0 and k == 0:
                        pe.wait_ge(consts.sem, consts.at(2))
                        pe.wait_ge(v_stored.sem, v_stored.at(NT))
                        pe.wait_ge(g_stored.sem, g_stored.at(NT // 2))
                    if k == 0:
                        pe.wait_ge(row_set.sem, row_set.at(16 * (h + 1)))
                        pe.wait_ge(kh1.sem, kh1.at(h + 1))
                    keys = slice(k * P, (k + 1) * P)
                    for half in range(2):
                        pe.matmul(Sb[k % 2][:, half, :], KHL[p][:, keys], QH[p][:, half * 512:(half + 1) * 512],
                                  start=True, stop=False)
                    for half in range(2):
                        m = pe.matmul(Sb[k % 2][:, half, :], KH1[p][:, keys],
                                      QL[p][:, half * 512:(half + 1) * 512], start=False, stop=True)
                    m.then_inc(s_filled.sem, 1)

                def attend(p, k, tiles):
                    for t in tiles:
                        m = pe.matmul(O(t), PB[:, k % NPB, t * P:(t + 1) * P], V1[p][:, k, :],
                                      start=(k == 0 and t % 4 == 0), stop=(k == KT - 1), skip_group_check=True)
                    return m

                def body(h, p, more=True, project_next=True):
                    i = 0
                    for k in range(KT):
                        if k + 1 < KT:
                            scores(h, p, k + 1)
                        elif more:
                            scores(h + 1, 1 - p, 0)
                        if project_next and k == KT - 2:
                            project(h + 2, p)
                        pe.wait_ge(exped.sem, exped.at(2 + KT * h + k + 1))
                        if k % (KT // 2) == 0:
                            pe.wait_ge(v_step.sem, v_step.at(VS * (2 * h + 1 + k // (KT // 2))))
                        if k == 0:
                            pe.wait_ge(o_evac.sem, o_evac.at(h + 1))
                        for part in range(4):
                            m = attend(p, k, range(2 * part, 2 * part + 2))
                            if part == 3:
                                m.then_inc(p_freed.sem, 1)
                            if more and part >= 4 - HALVES.get(k, 0):
                                max_scores(h + 1, 1 - p, i)
                                i += 1
                            if more and k == 5 and part == 2:
                                max_turn(h + 1, 1 - p)

                pe.sem_inc(p_freed.sem, NPB)
                project(0, 0)
                for n in range(2):
                    values(n)
                for t in range(NT):
                    pe.wait_ge(m_freed.sem, m_freed.at(max(2 * t - 1, 1)))
                    if t == 1:
                        pe.wait_ge(g_stored.sem, g_stored.at(NT // 2))
                    for half in range(2):
                        m = pe.matmul(first_scores(t)[:, half, :], QH[0][:, t * P:(t + 1) * P],
                                      KHL[0][:, half * 512:(half + 1) * 512], start=True, stop=True)
                    m.then_inc(m_filled.sem, 2)
                    if t + 2 < NT:
                        values(t + 2)
                max_turn(0, 0)
                project(1, 1)
                scores(0, 0, 0)
                with pe.Fori(0, H // 2 - 1) as i:
                    body(2 * i, 0)
                    body(2 * i + 1, 1)
                body(H - 2, 0, project_next=False)
                body(H - 1, 1, more=False, project_next=False)

                pe.wait_ge(exped.sem, exped.at(2 + KT * H))
                pe.wait_ge(m_freed.sem, m_freed.at(R * H))

                def a_turn(n):
                    pe.wait_ge(o_added.sem, o_added.at(NT * (H + 1) + n + 1))
                    if n >= 4:
                        pe.wait_ge(a_copied.sem, a_copied.at(n - 3))
                    for ec in range(NEC):
                        m = turn(pe, ps[:, 2 + n % 4, ec * P:(ec + 1) * P],
                                 A[:, n].rearrange("p e d -> p (e d)")[:, ec * P:(ec + 1) * P], ident[:])
                    m.then_inc(a_turned.sem, 1)

                a_turn(0)
                for n in range(NT):
                    if n + 1 < NT:
                        a_turn(n + 1)
                    pe.wait_ge(a_copied.sem, a_copied.at(n + 1))
                    for ec in range(NEC):
                        m = pe.matmul(ps[:, n // 4, (n % 4) * P:(n % 4 + 1) * P], AT[:, ec, n * P:(n + 1) * P],
                                      WOF[:, ec, :], start=ec == 0, stop=ec == NEC - 1)
                    m.then_inc(projected.sem, 1)

            @block.scalar
            def _(a):
                layernorm_scalar(a, S, L, ident)
                for n in range(2):
                    a.wait_ge(turned.sem, turned.at(n + 1))
                    a.activation(XH[:, n * 512:(n + 1) * 512], ps[:, n, :], ACT.Copy).then_inc(hi.sem, 1)
                a.activation(L["warm"][:], ident[:, 0:1], ACT.Exp)
                for n in range(1, NT // 2, 2):
                    a.wait_ge(gated.sem, gated.at(2 * n + 2))
                    a.activation(*gates_of_bank(n), ACT.Copy).then_inc(g_stored.sem, 1)

                def q_high(h, p):
                    a.wait_ge(m_filled.sem, m_filled.at(R * h + 1))
                    a.activation(QH[p][0:DH, :], M1[0:DH], ACT.Copy, scale=scale)
                    a.activation(QH[p][DH:2 * DH, :], M1[0:DH], ACT.Copy, scale=scale)

                def k_high(p):
                    a.activation(KHL[p][0:DH, :], M1[DH:2 * DH], ACT.Copy).then_inc(qk_hi.sem, 1)

                def k_high_again(h, p):
                    a.wait_ge(qk_hi.sem, qk_hi.at(h + 1))
                    a.activation(KH1[p][0:DH, :], KHL[p][0:DH, :].bitcast(F32), ACT.Copy).then_inc(kh1.sem, 1)

                def row(h, p, reused=True):
                    a.wait_ge(m_filled.sem, m_filled.at(R * (h + 1)))
                    if reused:
                        a.wait_ge(row_set.sem, row_set.at(16 * h))
                    a.activation(ROW[p][:], M[0:NT, 0, 0:P], ACT.Copy).then_inc(row_made.sem, 1)
                    a.wait_ge(row_made.sem, row_made.at(h + 1))
                    a.sem_inc(m_freed.sem, 1)

                def exp(h, k):
                    a.wait_ge(s_filled.sem, s_filled.at(KT * h + k + 1))
                    a.wait_ge(p_freed.sem, p_freed.at(KT * h + k + 1))
                    a.activation(PB[:, k % NPB, :], Sb[k % 2].rearrange("p s c -> p (s c)"), ACT.Exp).then_inc(
                        exped.sem, 1)

                def evacuate(h, p):
                    a.wait_ge(p_freed.sem, p_freed.at(NPB + KT * (h + 1)))
                    a.wait_ge(o_added.sem, o_added.at(NT * (h + 1)))
                    for half in range(2):
                        m = a.activation(OS[p][:, 4 * half:4 * half + 4, :].rearrange("p t d -> p (t d)"),
                                         ps[:, 6 + half, 0:4 * (DH + 1)], ACT.Copy)
                    m.then_inc(o_evac.sem, 1)

                def body(h, p, more=True, project_next=True):
                    exp(h, 1)
                    exp(h, 2)
                    if more:
                        k_high_again(h + 1, 1 - p)
                    for k in range(3, KT):
                        exp(h, k)
                        if more and k == KT - 2:
                            row(h + 1, 1 - p)
                    if project_next:
                        q_high(h + 2, p)
                        k_high(p)
                    if more:
                        exp(h + 1, 0)
                    evacuate(h, p)

                def store_values(tiles):
                    for n in tiles:
                        a.wait_ge(valued.sem, valued.at(n + 1))
                        a.activation(PROJV[:, n].rearrange("p e d -> p (e d)"), ps[:, 2 + n % 2, :], ACT.Copy).then_inc(
                            v_stored.sem, 1)

                a.sem_inc(exped.sem, 2)
                a.sem_inc(o_evac.sem, 1)
                q_high(0, 0)
                k_high(0)
                store_values(range(2))
                a.wait_ge(g_stored.sem, g_stored.at(NT // 2))
                gates = GT[:, 0].rearrange("p (n h) e -> p n (h e)", n=NT)
                a.activation(SG[:], gates, ACT.Abs).then_inc(sigmoid_step.sem, 1)
                a.wait_ge(sigmoid_step.sem, sigmoid_step.at(1))
                a.activation(SG[:], SG[:], ACT.Exp, scale=-1.0).then_inc(sigmoid_step.sem, 1)
                store_values(range(2, 4))
                a.wait_ge(sigmoid_step.sem, sigmoid_step.at(2))
                a.activation(SG[:], SG[:], ACT.Ln, bias=1.0).then_inc(sigmoid_step.sem, 1)
                a.activation(L["warm"][:], ident[:, 0:1], ACT.Exp)
                store_values(range(4, NT - 2))
                a.wait_ge(log_sigmoid.sem, log_sigmoid.at(1))
                a.activation(SG[:], SG[:], ACT.Exp).then_inc(sigmoid.sem, 1)
                store_values(range(NT - 2, NT))
                k_high_again(0, 0)
                row(0, 0, reused=False)
                q_high(1, 1)
                k_high(1)
                exp(0, 0)
                with a.Fori(0, H // 2 - 1) as i:
                    body(2 * i, 0)
                    body(2 * i + 1, 1)
                body(H - 2, 0, project_next=False)
                body(H - 1, 1, more=False, project_next=False)

                a.wait_ge(p_freed.sem, p_freed.at(NPB + KT * H))
                for n in range(NT):
                    a.wait_ge(a_turned.sem, a_turned.at(n + 1))
                    a.activation(AT[:, :, n * P:(n + 1) * P], ps[:, 2 + n % 4, :].rearrange("p (e q) -> p e q", e=NEC),
                                 ACT.Copy).then_inc(a_copied.sem, 1)

            @block.vector
            def _(v):
                chain = S("dve_chain")
                layernorm_vector(v, S, X, L)
                v.tensor_copy(CNT[:].rearrange("p k g e -> p (k g) e"), over_mid(later[:], 2 * G)).then_inc(
                    cnt_set.sem, 1)
                for n in range(2):
                    v.wait_ge(hi.sem, hi.at(n + 1))
                    v.tensor_tensor(XL[:, n * 512:(n + 1) * 512], ps[:, n, :],
                                    XH[:, n * 512:(n + 1) * 512].bitcast(F32), ALU.subtract).then_inc(lo.sem, 1)
                for n in range(0, NT // 2, 2):
                    v.wait_ge(gated.sem, gated.at(2 * n + 2))
                    v.tensor_copy(*gates_of_bank(n)).then_inc(g_stored.sem, 1)
                v.wait_ge(g_stored.sem, g_stored.at(NT // 2))
                v.wait_ge(cnt_set.sem, cnt_set.at(1))
                compare_all(v, 0)

                v.sem_inc(o_added.sem, 2 * NT)

                def low(h, p):
                    v.wait_ge(qk_hi.sem, qk_hi.at(h + 1))
                    v.scalar_tensor_tensor(QL[p][0:DH, :], M1[0:DH], scale, QH[p][0:DH, :].bitcast(F32),
                                           ALU.mult, ALU.subtract)
                    v.tensor_tensor(KHL[p][DH:2 * DH, :], M1[DH:2 * DH], KHL[p][0:DH, :].bitcast(F32),
                                    ALU.subtract).then_inc(m_freed.sem, 1)

                def maximum(h, p, i):
                    v.wait_ge(m_filled.sem, m_filled.at(R * h + 2 + i))
                    v.tensor_reduce(NH[p][:, i // 2, i % 2:i % 2 + 1], M[:, i % 2, :], AX_X,
                                    ALU.max).then_inc(m_freed.sem, 1)

                def maxima(h, p):
                    v.wait_ge(m_freed.sem, m_freed.at(R * h + 1 + 2 * NT))
                    v.tensor_reduce(NM[p][:], NH[p][:], AX_X, ALU.max, negate=True).then_inc(max_ready.sem, 1)

                def weights(h, p):
                    v.wait_ge(o_evac.sem, o_evac.at(h + 2))
                    v.reciprocal(RDN[:], OS[p][:, :, DH]).then_inc(o_rden.sem, 1)
                    v.wait_ge(o_rden.sem, o_rden.at(h + 1))
                    before = CNT[:, 1].rearrange("p (n h) e -> p n h e", n=NT)[:, :, bass.ds(h, 1), :].rearrange(
                        "p n o e -> p n (o e)")
                    v.scalar_tensor_tensor(MW[:], before, 2.0, over(RDN[:], E), ALU.is_lt, ALU.mult).then_inc(o_weight.sem, 1)
                    v.wait_ge(o_weight.sem, o_weight.at(h + 1))

                def product(h, p, t):
                    v.wait_ge(o_added.sem, o_added.at(NT * (h + 2) + t - 1))
                    v.tensor_tensor(OP[t % 2][:], over_mid(OS[p][:, t, 0:DH], E), over(MW[:, t, :], DH),
                                    ALU.mult).then_inc(o_prod.sem, 1)

                def added(h, t):
                    v.wait_ge(o_prod.sem, o_prod.at(NT * h + t + 1))
                    v.tensor_tensor(A[:, t], A[:, t], OP[t % 2][:], ALU.add).then_inc(o_added.sem, 1)

                def sum_steps(h, p):
                    yield lambda: product(h, p, 0)
                    for t in range(NT):
                        if t + 1 < NT:
                            yield lambda t=t: product(h, p, t + 1)
                        yield lambda t=t: added(h, t)

                def body(h, p):
                    low(h + 1, 1 - p)
                    maximum(h + 1, 1 - p, 0)
                    maximum(h + 1, 1 - p, 1)
                    weights(h - 1, 1 - p)
                    steps = sum_steps(h - 1, 1 - p)
                    for i in range(2, 2 * NT):
                        if i in SUMS_BEFORE:
                            next(steps)()
                        maximum(h + 1, 1 - p, i)
                    maxima(h + 1, 1 - p)
                    for step in steps:
                        step()

                low(0, 0)
                for t in range(NT):
                    v.wait_ge(m_filled.sem, m_filled.at(2 * t + 3))
                    v.tensor_reduce(NM[0][:, t:t + 1], first_scores(t).rearrange("p s c -> p (s c)"), AX_X, ALU.max,
                                    negate=True).then_inc(m_freed.sem, 2)
                    if t < NEAR:
                        count(v, chain, CNT[:, 0], t + 1)
                    if t == NT // 2 - 2:
                        v.wait_ge(sigmoid_step.sem, sigmoid_step.at(3))
                        v.scalar_tensor_tensor(SG[:], GT[:, 0].rearrange("p (n h) e -> p n (h e)", n=NT), 0.0, SG[:],
                                               ALU.min, ALU.subtract).then_inc(log_sigmoid.sem, 1)
                    if t == NT // 2:
                        v.wait_ge(counted.sem, counted.at(1))
                        link(v, chain, v.tensor_tensor(CNT[:, 0], CNT[:, 0], CNTP[:], ALU.add))
                        v.wait_ge(sigmoid.sem, sigmoid.at(1))
                        v.scalar_tensor_tensor(MIX[:].rearrange("p n h e -> p n (h e)"),
                                               CNT[:, 0].rearrange("p (n h) e -> p n (h e)", n=NT), 2.0, SG[:],
                                               ALU.is_lt, ALU.mult).then_inc(mixed.sem, 1)
                v.wait_ge(m_freed.sem, m_freed.at(2 * NT + 1))
                v.sem_inc(max_ready.sem, 1)
                compare_all(v, 1)
                low(1, 1)
                for i in range(2 * NT):
                    maximum(1, 1, i)
                maxima(1, 1)
                for d in range(1, E):
                    count(v, chain, CNT[:, 1], d)
                v.wait_ge(consts.sem, consts.at(3))
                with v.Fori(0, H // 2 - 1) as i:
                    body(2 * i + 1, 1)
                    body(2 * i + 2, 0)
                for h in range(H - 2, H):
                    weights(h, h % 2)
                    for step in sum_steps(h, h % 2):
                        step()

                for n in range(2):
                    v.wait_ge(projected.sem, projected.at(4 * n + 4))
                    xs = X[:, 4 * n:4 * n + 4, :]
                    v.tensor_tensor(xs, ps[:, n, :].rearrange("p (n c) -> p n c", n=4), xs, ALU.add)
        S.close(var_ready=1, std_ready=1, normed=2, turned=2, split_hi=2, split_lo=2,
                valued=NT, gated=NT, v_stored=NT, g_stored=NT // 2, cnt_set=1, gates_compared=2 * (E - 1), gates_counted=1, sigmoid_step=3,
                log_sigmoid=1, sigmoid=1, mixed=1)
        S.close(w_staged0=8 * H, w_staged1=8 * H, head_consts=3, m_filled=R * H, m_freed=R * H, qk_hi=H, kh1_ready=H,
                row_made=H, max_ready=H, row_set=16 * H, s_filled=KT * H, exped=2 + KT * H, p_freed=NPB + KT * H,
                o_evac=H + 1, v_step=2 * VS * H, o_rden=H, o_weight=H, o_prod=NT * H, o_added=NT * (H + 2))
        S.close(a_turned=NT, a_copied=NT, projected=NT)


_INS = ["L0_attn_a_x", "L0_attn_a_Wq", "L0_attn_a_Wk", "L0_attn_a_Wv", "L0_attn_a_Wo", "L0_attn_a_q_gamma",
        "L0_attn_a_k_gamma", "L0_attn_b_wq", "L0_attn_b_wk", "L0_attn_b_wv", "L0_attn_b_wo", "L0_ffn_Wq",
        "L0_ffn_Wk", "L0_ffn_Wv", "L0_ffn_Ws", "L0_ffn_Wd", "L0_ffn_Wo"]


def rope_tables(T, head_dim):
    exponent = np.arange(0, head_dim, 2, dtype=np.float32) / np.float32(head_dim)
    inv_freq = (np.float32(1.0) / np.power(np.float32(1000000.0), exponent)).astype(np.float32)
    angles = np.outer(np.arange(T, dtype=np.float32), inv_freq).astype(np.float32)
    return np.cos(angles.astype(np.float64)).astype(np.float32), np.sin(angles.astype(np.float64)).astype(np.float32)


def kernel(**inputs):
    import concourse.bacc as _bacc
    from concourse.bass_utils import run_bass_kernel_spmd as _run

    nc = _bacc.Bacc("TRN2", target_bir_lowering=False, num_devices=1)
    arrays, args = {}, {}
    for name in _INS:
        a = np.ascontiguousarray(inputs[name])
        arrays[f"in_{name}_dram"] = a
        args[name] = nc.dram_tensor(f"in_{name}_dram", a.shape, mybir.dt.from_np(a.dtype), kind="ExternalInput").ap()
    shape = args["L0_attn_a_x"].shape
    cos, sin = rope_tables(shape[1], 32)
    for name, a in (("rope_cos", cos), ("rope_sin", sin)):
        arrays[f"in_{name}_dram"] = a
        args[name] = nc.dram_tensor(f"in_{name}_dram", a.shape, mybir.dt.from_np(a.dtype), kind="ExternalInput").ap()
    out = nc.dram_tensor("out_0_dram", shape, F32, kind="ExternalOutput").ap()
    build(nc, args, out)
    r = _run(nc, [arrays], core_ids=[0])
    return r.results[0]["out_0_dram"]
```
